# Optimizing a Trainium2 kernel written in Bass

```python
import numpy as np
import jax
import jax.numpy as jnp

def _softmax(x, axis=-1):
    return jax.nn.softmax(x, axis=axis)

def _gelu(x):
    return jax.nn.gelu(x, approximate=True)

def _silu(x):
    return jax.nn.silu(x)

def _sigmoid(x):
    return jax.nn.sigmoid(x)

def _layernorm(x, axis=-1, eps=1e-05):
    m = jnp.mean(x, axis=axis, keepdims=True)
    v = jnp.var(x, axis=axis, keepdims=True)
    return (x - m) / jnp.sqrt(v + eps)

def _scatter_add(tgt, idx, src, axis=0):
    return tgt.at[idx].add(src)

def _segment_sum(src, seg, n):
    return jax.ops.segment_sum(src, seg, n)
kernel_name = 'mk_sandwich_d1_jaxref_r8_dbd242'

def setup_inputs(seed: int=0):
    np.random.seed(seed)
    _w = jnp.asarray

    def _L0_attn_setup():
        import jax, jax.numpy as jnp
        import numpy as np
        B, T, C = (2, 256, 128)
        LAT = 32
        N_HEAD = 16
        HEAD_DIM = C // N_HEAD
        SCALE = 1.0 / np.sqrt(HEAD_DIM).astype(np.float32)
        key = jax.random.key(seed)
        ks = jax.random.split(key, 9)
        s_in = 0.02
        return {'x': jax.random.normal(ks[0], (B, T, C), dtype=jnp.float32), 'wq_lat': jax.random.normal(ks[1], (C, LAT), dtype=jnp.float32) * s_in, 'wk_lat': jax.random.normal(ks[2], (C, LAT), dtype=jnp.float32) * s_in, 'wv_lat': jax.random.normal(ks[3], (C, LAT), dtype=jnp.float32) * s_in, 'wq_heads': jax.random.normal(ks[4], (LAT, C), dtype=jnp.float32) * s_in, 'wk_heads': jax.random.normal(ks[5], (LAT, C), dtype=jnp.float32) * s_in, 'wv_heads': jax.random.normal(ks[6], (LAT, C), dtype=jnp.float32) * s_in, 'w_proj': jax.random.normal(ks[7], (C, C), dtype=jnp.float32) * s_in, 'b_proj': jnp.zeros((C,), dtype=jnp.float32)}
    _L0_attn_in = _L0_attn_setup()

    def _L0_ffn_setup():
        import jax, jax.numpy as jnp
        import numpy as np
        EPS = 1e-06
        LN_EPS = 1e-05

        def _absmean_core(W):
            gamma = jnp.mean(jnp.abs(W)) + EPS
            Ws = W / gamma
            Wq = jnp.sign(Ws) * jnp.minimum(jnp.round(jnp.abs(Ws)), 1.0)
            return (Wq, gamma)

        @jax.custom_vjp
        def absmean(W):
            return _absmean_core(W)[0]

        def _absmean_fwd(W):
            Wq, gamma = _absmean_core(W)
            return (Wq, gamma)

        def _absmean_bwd(gamma, g):
            return (g / gamma,)
        absmean.defvjp(_absmean_fwd, _absmean_bwd)

        def layernorm(x, w, b, eps=LN_EPS):
            mu = jnp.mean(x, axis=-1, keepdims=True)
            var = jnp.mean((x - mu) ** 2, axis=-1, keepdims=True)
            return (x - mu) * jax.lax.rsqrt(var + eps) * w + b
        key = jax.random.key(seed)
        k1, k2, k3 = jax.random.split(key, 3)
        d, h = (128, 512)
        B, T = (8, 256)
        return {'x': jax.random.normal(k1, (B, T, d), jnp.float32), 'W_fc': jax.random.normal(k2, (h, d), jnp.float32), 'ln_w': jnp.ones((h,), jnp.float32), 'ln_b': jnp.zeros((h,), jnp.float32), 'W_proj': jax.random.normal(k3, (d, h), jnp.float32)}
    _L0_ffn_in = _L0_ffn_setup()
    _d = {'L0_attn_x': _L0_attn_in['x'], 'L0_attn_wq_lat': _L0_attn_in['wq_lat'], 'L0_attn_wk_lat': _L0_attn_in['wk_lat'], 'L0_attn_wv_lat': _L0_attn_in['wv_lat'], 'L0_attn_wq_heads': _L0_attn_in['wq_heads'], 'L0_attn_wk_heads': _L0_attn_in['wk_heads'], 'L0_attn_wv_heads': _L0_attn_in['wv_heads'], 'L0_attn_w_proj': _L0_attn_in['w_proj'], 'L0_attn_b_proj': _L0_attn_in['b_proj'], 'L0_ffn_W_fc': _L0_ffn_in['W_fc'], 'L0_ffn_ln_w': _L0_ffn_in['ln_w'], 'L0_ffn_ln_b': _L0_ffn_in['ln_b'], 'L0_ffn_W_proj': _L0_ffn_in['W_proj']}
    _x0 = _d['L0_attn_x']
    _d['L0_attn_x'] = jax.random.normal(jax.random.fold_in(jax.random.key(seed), 1), (2, 1024, 128), dtype=_x0.dtype)
    del _x0
    return _d

def reference(L0_attn_x, L0_attn_wq_lat, L0_attn_wk_lat, L0_attn_wv_lat, L0_attn_wq_heads, L0_attn_wk_heads, L0_attn_wv_heads, L0_attn_w_proj, L0_attn_b_proj, L0_ffn_W_fc, L0_ffn_ln_w, L0_ffn_ln_b, L0_ffn_W_proj):

    def _L0_attn_ref(x, wq_lat, wk_lat, wv_lat, wq_heads, wk_heads, wv_heads, w_proj, b_proj):
        import jax, jax.numpy as jnp
        import numpy as np
        B, T, C = (2, 256, 128)
        LAT = 32
        N_HEAD = 16
        HEAD_DIM = C // N_HEAD
        SCALE = 1.0 / np.sqrt(HEAD_DIM).astype(np.float32)
        Bx, Tx, Cx = x.shape
        q = x @ wq_lat @ wq_heads
        k = x @ wk_lat @ wk_heads
        v = x @ wv_lat @ wv_heads
        q = q.reshape(Bx, Tx, N_HEAD, HEAD_DIM).transpose(0, 2, 1, 3)
        k = k.reshape(Bx, Tx, N_HEAD, HEAD_DIM).transpose(0, 2, 1, 3)
        v = v.reshape(Bx, Tx, N_HEAD, HEAD_DIM).transpose(0, 2, 1, 3)
        att = jnp.einsum('bhqd,bhkd->bhqk', q, k) * SCALE
        causal = jnp.tril(jnp.ones((Tx, Tx), dtype=bool))
        att = jnp.where(causal[None, None], att, -jnp.inf)
        att = jax.nn.softmax(att, axis=-1)
        y = jnp.einsum('bhqk,bhkd->bhqd', att, v)
        y = y.transpose(0, 2, 1, 3).reshape(Bx, Tx, Cx)
        return y @ w_proj + b_proj

    def _L0_ffn_ref(x, W_fc, ln_w, ln_b, W_proj):
        import jax, jax.numpy as jnp
        import numpy as np
        EPS = 1e-06
        LN_EPS = 1e-05

        def _absmean_core(W):
            gamma = jnp.mean(jnp.abs(W)) + EPS
            Ws = W / gamma
            Wq = jnp.sign(Ws) * jnp.minimum(jnp.round(jnp.abs(Ws)), 1.0)
            return (Wq, gamma)

        @jax.custom_vjp
        def absmean(W):
            return _absmean_core(W)[0]

        def _absmean_fwd(W):
            Wq, gamma = _absmean_core(W)
            return (Wq, gamma)

        def _absmean_bwd(gamma, g):
            return (g / gamma,)
        absmean.defvjp(_absmean_fwd, _absmean_bwd)

        def layernorm(x, w, b, eps=LN_EPS):
            mu = jnp.mean(x, axis=-1, keepdims=True)
            var = jnp.mean((x - mu) ** 2, axis=-1, keepdims=True)
            return (x - mu) * jax.lax.rsqrt(var + eps) * w + b
        h = jnp.einsum('btd,hd->bth', x, absmean(W_fc))
        h = jax.nn.gelu(h, approximate=False)
        h = layernorm(h, ln_w, ln_b)
        return jnp.einsum('bth,dh->btd', h, absmean(W_proj))
    x = L0_attn_x
    x = x + _layernorm(_L0_attn_ref(_layernorm(x, axis=-1), L0_attn_wq_lat, L0_attn_wk_lat, L0_attn_wv_lat, L0_attn_wq_heads, L0_attn_wk_heads, L0_attn_wv_heads, L0_attn_w_proj, L0_attn_b_proj), axis=-1)
    x = x + _layernorm(_L0_ffn_ref(_layernorm(x, axis=-1), L0_ffn_W_fc, L0_ffn_ln_w, L0_ffn_ln_b, L0_ffn_W_proj), axis=-1)
    return x

_drawn_inputs = setup_inputs


def setup_inputs(seed=0):
    import zlib

    import numpy as np

    out = dict(_drawn_inputs(seed))
    spreads = {'L0_attn_b_proj': (0.0, 0.1), 'L0_ffn_ln_w': (1.0, 0.2), 'L0_ffn_ln_b': (0.0, 0.1)}
    factors = {'L0_attn_wq_lat': 8.0,
     'L0_attn_wk_lat': 8.0,
     'L0_attn_wv_lat': 8.0,
     'L0_attn_wq_heads': 8.0,
     'L0_attn_wk_heads': 8.0,
     'L0_attn_wv_heads': 8.0,
     'L0_attn_w_proj': 8.0}
    for name, (base, spread) in spreads.items():
        noise = np.random.default_rng([zlib.crc32(name.encode()), seed]).standard_normal(out[name].shape)
        drawn = base * np.exp(spread * noise) if base else spread * noise
        out[name] = jnp.asarray(drawn.astype(out[name].dtype))
    for name, factor in factors.items():
        out[name] = (out[name] * factor).astype(out[name].dtype)
    return out
```

```python
from contextlib import ExitStack

import concourse.bass as bass
from concourse import mybir

ALU = mybir.AluOpType
ACT = mybir.ActivationFunctionType
AX = mybir.AxisListType
F32 = mybir.dt.float32
BF16 = mybir.dt.bfloat16
U32 = mybir.dt.uint32

P = 128
B, T, C = 2, 1024, 128
LAT = 32
NH, HD = 16, 8
HID = 512
NT = T // P
QUAD = 4
NQ = NH // QUAD
HALF = T // 2
SCALE = HD ** -0.5
LN_EPS = 1e-5
GAMMA_EPS = 1e-6
MASKED = -3.0e38
ROWS = 96
ZERO_ROW = 48
SHIFT_ROW = 64
STACKS = 3
PGROUPS = 4

Q_PARTS = (0, 0, 0, 1, 1, 2)
K_PARTS = (0, 1, 2, 0, 1, 0)

def score_groups():
    nb = HALF // P
    groups = []
    for c in range(2):
        for kb in range(nb * c):
            groups.append((c, [(kb, HALF * c, HALF, 0)], 1))
        d, e = nb * c, HALF * (c + 1)
        groups.append((c, [(d, P * d, HALF, 0)], 1))
        groups.append((c, [(d + 1, P * (d + 1), 3 * P, P), (d + 3, P * (d + 3), P, 0)], 1))
        groups.append((c, [(d + 2, P * (d + 2), 2 * P, 0)], 2))
    return groups


GROUPS = score_groups()
UNITS = [(g, tuple(range(i, i + GROUPS[g][2]))) for g in range(len(GROUPS)) for i in range(0, QUAD, GROUPS[g][2])]
NU = len(UNITS)
GROUP_END = [max(u for u, (g, _) in enumerate(UNITS) if g == j) for j in range(len(GROUPS))]
HALF_END = [max(j for j, x in enumerate(GROUPS) if x[0] == c) for c in range(2)]

MAX_TILES = [(0, (0, 1, 2, 3)), (1, (0, 1, 2, 3)), (2, (0, 1)), (2, (2, 3)), (3, (0, 1)), (3, (2, 3))]
MAX_TILES += [(i, (h,)) for i in range(4, NT) for h in range(QUAD)]

NORMS = 5
PV_LAG = 5
STEPS = NQ * NU
TAIL = 12


def schedule():
    pv_at, evac_at, tiles_at = {}, {}, {}
    for n in range(NQ):
        for g in range(len(GROUPS)):
            pv_at.setdefault(n * NU + GROUP_END[g] + PV_LAG, []).append((n, g))
        for c in range(2):
            done = n * NU + GROUP_END[HALF_END[c]] + PV_LAG
            evac_at[min(done + 1, STEPS + TAIL - 1)] = (n, c)
            tiles_at.setdefault(done + 4, []).append(("o", n, c))
        if n + 1 < NQ:
            for k in range(len(MAX_TILES)):
                tiles_at.setdefault(n * NU + k * 30 // len(MAX_TILES), []).append(("max", n + 1, k))
            tiles_at.setdefault(n * NU + 32, []).append(("ms", n + 1, 0))
    return pv_at, evac_at, tiles_at


PV_AT, EVAC_AT, TILES_AT = schedule()


def tile_order():
    order = [("wsum", 0, 0, 0), ("c2", 0, 0, 0)]
    for b in range(B):
        order += [(k, b, 0, 0) for k in ("xT", "lat", "q", "k", "v")]
        order += [("max", b, 0, k) for k in range(len(MAX_TILES))] + [("ms", b, 0, 0)]
        for s in range(STEPS + TAIL):
            order += [(kind, b, n, k) for kind, n, k in TILES_AT.get(s, ())]
        order += [("yT", b, 0, 0), ("proj", b, 0, 0), ("x1T", b, 0, 0)]
        order += [("ffn1", b, 0, k) for k in range(4)] + [("hT", b, 0, k) for k in range(4)] + [("ffn2", b, 0, 0)]
    return {name: i for i, name in enumerate(order)}


TILE_NO = tile_order()


def max_place(i, j):
    return (P * (i + 1) if i < 2 else HALF) * j


def stack_loads(b, n):
    return b * len(range(n % STACKS, NQ, STACKS)) + n // STACKS + 1


def tile_frees(slot, name):
    return (TILE_NO[name] - slot) // 2 + 1


def block_kernel(nc, x, w_lat, w_heads, w_proj, b_proj, w_fc_t, ln_w, ln_b, w_out_t, out):
    with ExitStack() as ctx:
        def sb(name, shape, dt=F32):
            return ctx.enter_context(nc.sbuf_tensor(name, shape, dt))

        def sem(name):
            return ctx.enter_context(nc.semaphore(name))

        ident = sb("ident", [P, P])
        ident16 = sb("ident16", [P, P], BF16)
        future = sb("future", [P, P], BF16)
        ones = sb("ones", [P, P])
        minus_half = sb("minus_half", [P, NT])
        wlat = sb("wlat", [P, 3 * LAT])
        wheads = sb("wheads", [3 * LAT, 3, C])
        wproj = sb("wproj", [C, C])
        bproj = sb("bproj", [P, C])
        wfc = sb("wfc", [P, HID])
        wfcq = sb("wfcq", [P, HID])
        wout = sb("wout", [P, HID // P, C])
        woutq = sb("woutq", [P, HID // P, C])
        woutl = sb("woutl", [P, HID // P, C])
        lnw = sb("lnw", [P, HID // P])
        lnb = sb("lnb", [P, HID // P])
        lnb_wide = sb("lnb_wide", [P, HID // P, P])
        c2 = sb("c2", [P, C])
        wstat = sb("wstat", [P, 8])
        wtmp = sb("wtmp", [P, HID])

        x_in = sb("x_in", [P, B, NT, C])
        xn = sb("xn", [P, NT, C])
        xnT = sb("xnT", [C, T])
        latT = sb("latT", [C, T])
        parts = sb("parts", [P, 2, 3, T], BF16)
        rest = sb("rest", [P, 2, T])
        v_aug = sb("v_aug", [P, NT, NH, 32])
        q_stack = sb("q_stack", [ROWS, STACKS, QUAD, T], BF16)
        k_stack = sb("k_stack", [ROWS, STACKS, QUAD, T], BF16)
        neg_max = sb("neg_max", [P, QUAD, NT])
        max_rest = sb("max_rest", [P, QUAD * NT])
        max_parts = sb("max_parts", [P, 3, QUAD * NT], BF16)
        max_rows = sb("max_rows", [3 * QUAD * NT, P], BF16)
        probs = sb("probs", [P, PGROUPS, QUAD * HALF])
        o_cols = sb("o_cols", [P, 2, HALF])
        o_recip = sb("o_recip", [P, 4, QUAD])
        y = sb("y", [P, NT, C])
        yT = latT
        x1 = sb("x1", [P, NT, C])
        x1n = xn
        x1T = xnT
        gelu = sb("gelu", [P, NT, HID])
        gT = sb("gT", [P, NT, HID // P, P])
        res = sb("res", [P, NT, C])
        stats = sb("stats", [P, NT, 6])
        mv = sb("mv", [P, NT, 2])
        veps = sb("veps", [P, NT])
        rstd = sb("rstd", [P, NT])

        ps = ctx.enter_context(nc.psum_tensor("ps", [P, 8, 512], F32))
        pv = ps[:, 7]

        def work(name):
            return ps[:, 2 * (TILE_NO[name] % 2):2 * (TILE_NO[name] % 2) + 2, :]

        def work_flat(name):
            return work(name).rearrange("p a n -> p (a n)")

        def scores_bank(u):
            return ps[:, 4 + u % 3]

        qk_parts = nc.dram_tensor("qk_parts", [B, 2, NH, 3, HD, T], BF16, kind="Internal").ap()

        weights_in = sem("weights_in")
        x_loaded = sem("x_loaded")
        heads_zeroed = sem("heads_zeroed")
        stacks_set = sem("stacks_set")
        consts_ready = sem("consts_ready")
        ident_ready = sem("ident_ready")
        vec_done = sem("vec_done")
        pool_done = sem("pool_done")
        act_done = sem("act_done")
        tile_ready = [sem("tile_ready0"), sem("tile_ready1")]
        tile_free = [sem("tile_free0"), sem("tile_free1")]
        wsum_in = sem("wsum_in")
        wide_ready = sem("wide_ready")
        wq_ready = sem("wq_ready")
        var_ready = sem("var_ready")
        rstd_ready = sem("rstd_ready")
        xn_ready = sem("xn_ready")
        part0_ready = sem("part0_ready")
        part1_ready = sem("part1_ready")
        part2_ready = sem("part2_ready")
        parts_out = sem("parts_out")
        stack_in = [sem(f"stack_in{i}") for i in range(STACKS)]
        max_split = sem("max_split")
        shift_in = sem("shift_in")
        scores_ready = sem("scores_ready")
        exp_done = sem("exp_done")
        masked = sem("masked")
        pv_done = sem("pv_done")
        o_ready = sem("o_ready")
        x1n_ready = sem("x1n_ready")
        gn_ready = sem("gn_ready")
        res_ready = sem("res_ready")
        stored = sem("stored")

        NDIAG = 6
        NG = len(GROUPS)

        def diag_count(n, g):
            before = [j for j in range(g + 1) if any(P * kb == q0 for kb, q0, _, _ in GROUPS[j][1])]
            return n * NDIAG + len(before)

        def is_diag(g):
            return any(P * kb == q0 for kb, q0, _, _ in GROUPS[g][1])

        def filled(eng, name):
            i = TILE_NO[name]
            eng.wait_ge(tile_ready[i % 2], i // 2 + 1)

        def emptied(eng, name):
            i = TILE_NO[name]
            eng.wait_ge(tile_free[i % 2], i // 2 + 1)

        def half_name(k):
            return "o", k // (2 * NQ), k // 2 % NQ, k % 2

        def release(ins, name):
            ins.then_inc(tile_free[TILE_NO[name] % 2], 1)

        def unit_count(b, n, u):
            return (b * NQ + n) * NU + u

        block = ctx.enter_context(nc.Block())

        @block.sync
        def _(sp):
            def load_x(b):
                sp.dma_start(x_in[:, b], x[b].rearrange("(t p) c -> p t c", p=P)).then_inc(x_loaded, 16)

            load_x(0)
            sp.wait_ge(heads_zeroed, 1)
            for i in range(3):
                sp.dma_start(wheads[LAT * i:LAT * (i + 1), i, :], w_heads[i]).then_inc(weights_in, 16)
                sp.dma_start(wlat[:, LAT * i:LAT * (i + 1)], w_lat[i]).then_inc(weights_in, 16)
            sp.dma_start(wproj[:, :], w_proj).then_inc(weights_in, 16)
            sp.dma_start(bproj[:, :], b_proj.rearrange("(a c) -> a c", a=1).to_broadcast([P, C])).then_inc(weights_in, 16)
            sp.dma_start(lnw[:, :], ln_w).then_inc(weights_in, 16)
            sp.dma_start(lnb[:, :], ln_b).then_inc(weights_in, 16)
            sp.dma_start(wfc[:, :], w_fc_t).then_inc(wsum_in, 16)
            sp.dma_start(wout[:, :, :], w_out_t.rearrange("(c p) d -> p c d", p=P)).then_inc(wsum_in, 16)
            sp.wait_ge(x_loaded, 16)
            load_x(1)

            def load_stacks(b, n):
                s = n % STACKS
                heads = slice(QUAD * n, QUAD * (n + 1))
                if n >= STACKS:
                    sp.wait_ge(scores_ready, unit_count(b, n - STACKS, NU))
                rows = qk_parts[b].rearrange("a h r d t -> a (r d) h t")
                for r, part in enumerate(Q_PARTS):
                    sp.dma_start(q_stack[HD * r:HD * (r + 1), s], rows[0, HD * part:HD * (part + 1), heads]
                                 ).then_inc(stack_in[s], 16)
                for r0, r1 in ((0, 3), (3, 5), (5, 6)):
                    sp.dma_start(k_stack[HD * r0:HD * r1, s], rows[1, 0:HD * (r1 - r0), heads]
                                 ).then_inc(stack_in[s], 16)
                sp.dma_start(q_stack[SHIFT_ROW:SHIFT_ROW + 3, s], k_stack[ZERO_ROW:ZERO_ROW + 3, s]
                             ).then_inc(stack_in[s], 16)

            def store_shift(b, n):
                emptied(sp, ("ms", b, n, 0))
                for r in range(3):
                    dst = q_stack[SHIFT_ROW + r:SHIFT_ROW + r + 1, n % STACKS].rearrange("a h (i q) -> a (h i) q", q=P)
                    sp.dma_start(dst, max_rows[QUAD * NT * r:QUAD * NT * (r + 1), :]).then_inc(shift_in, 16)

            for b in range(B):
                for a in range(2):
                    for r, ready in ((0, part0_ready), (1, part1_ready), (2, part2_ready)):
                        sp.wait_ge(ready, 2 * b + a + 1)
                        sp.dma_start(qk_parts[b, a, :, r], parts[:, a, r, :]
                                     ).then_inc(parts_out, 16)
                sp.wait_ge(parts_out, 16 * 6 * (b + 1))
                if b == 0:
                    sp.wait_ge(stacks_set, 2)
                load_stacks(b, 0)
                load_stacks(b, 1)
                store_shift(b, 0)
                for n in range(NQ - 1):
                    if n + 2 < NQ:
                        load_stacks(b, n + 2)
                    store_shift(b, n + 1)
                sp.wait_ge(res_ready, b + 1)
                sp.dma_start(out[b].rearrange("(t p) c -> p t c", p=P), res[:, :, :]).then_inc(stored, 16)
            sp.wait_ge(stored, 16 * B)

        @block.gpsimd
        def _(pool):
            nc.gpsimd.memset(wheads[:, :, :], 0.0).then_inc(heads_zeroed, 1)
            nc.gpsimd.memset(minus_half[:, :], -0.5)
            nc.gpsimd.memset(ident[:, :], 0.0)
            nc.gpsimd.memset(ident16[:, :], 0.0)
            nc.gpsimd.memset(future[:, :], 0.0).then_inc(pool_done, 1)
            pool.wait_ge(pool_done, 1)
            for t in (ident, ident16):
                nc.gpsimd.affine_select(out=t[:, :], in_=t[:, :], compare_op=ALU.not_equal, fill=1.0, base=0,
                                        pattern=[[-1, P]], channel_multiplier=1).then_inc(ident_ready, 1)
            nc.gpsimd.affine_select(out=future[:, :], in_=future[:, :], compare_op=ALU.is_ge, fill=MASKED, base=0,
                                    pattern=[[-1, P]], channel_multiplier=1).then_inc(ident_ready, 1)

            nc.gpsimd.memset(q_stack[:, :, :, :].rearrange("r s h t -> r (s h t)").bitcast(U32), 0
                             ).then_inc(stacks_set, 1)

            def inverse_std(k):
                pool.wait_ge(var_ready, k + 1)
                nc.gpsimd.tensor_tensor(rstd[:, :], veps[:, :], minus_half[:, :], ALU.pow).then_inc(rstd_ready, 1)

            def part2(b, a):
                pool.wait_ge(part1_ready, 2 * b + a + 1)
                nc.gpsimd.tensor_tensor(parts[:, a, 2, :], rest[:, a, :], parts[:, a, 1, :],
                                        ALU.subtract).then_inc(part2_ready, 1)

            def mask(b, n, g):
                _, pieces, per = GROUPS[g]
                pool.wait_ge(exp_done, unit_count(b, n, GROUP_END[g] + 1))
                buf = probs[:, ((b * NQ + n) * NG + g) % PGROUPS, :]
                if per == 2:
                    v = buf[:, 0:QUAD * 2 * P].rearrange("p (h q) -> p h q", h=QUAD)[:, :, 0:P]
                    pattern = [[0, QUAD], [1, P]]
                elif len(pieces) == 2:
                    v = buf.rearrange("p (h q) -> p h q", h=QUAD)[:, :, 0:2 * P]
                    pattern = [[0, QUAD], [0, 2], [1, P]]
                else:
                    v = buf.rearrange("p (h q) -> p h q", h=QUAD)[:, :, 0:P]
                    pattern = [[0, QUAD], [1, P]]
                nc.gpsimd.affine_select(out=v, in_=v, compare_op=ALU.is_ge, fill=0.0, base=0,
                                        pattern=pattern, channel_multiplier=-1).then_inc(masked, 1)

            for b in range(B):
                inverse_std(NORMS * b)
                part2(b, 0)
                part2(b, 1)
                for n in range(NQ):
                    for g in range(NG):
                        if is_diag(g):
                            mask(b, n, g)
                for k in range(1, NORMS):
                    inverse_std(NORMS * b + k)

        @block.tensor
        def _(pe):
            def claim(name):
                i = TILE_NO[name]
                if i >= 2:
                    pe.wait_ge(tile_free[i % 2], i // 2)
                return work_flat(name)

            def fill_done(ins, name):
                ins.then_inc(tile_ready[TILE_NO[name] % 2], 1)

            def turn_tiles(name, src):
                w = claim(name)
                for t in range(NT):
                    mm = pe.transpose(w[:, P * t:P * (t + 1)], src[:, t, :], ident[:, :])
                fill_done(mm, name)

            def project(name, lhs, rhs):
                w = claim(name)
                m = lhs.shape[1]
                for c in range(2):
                    mm = pe.matmul(w[0:m, HALF * c:HALF * (c + 1)], lhs, rhs[:, HALF * c:HALF * (c + 1)],
                                   start=True, stop=True)
                fill_done(mm, name)

            def max_tile(b, n, k):
                name = ("max", b, n, k)
                i, heads = MAX_TILES[k]
                s = n % STACKS
                if k == 0:
                    pe.wait_ge(stack_in[s], 160 * stack_loads(b, n))
                w = claim(name)
                width = P * (i + 1)
                for j, h in enumerate(heads):
                    at = max_place(i, j)
                    lhs = q_stack[:, s, h, P * i:P * (i + 1)]
                    for k0 in range(0, width, 512):
                        kw = min(512, width - k0)
                        last = k0 + kw == width
                        mm = pe.matmul(w[:, at + k0:at + k0 + kw], lhs, k_stack[:, s, h, k0:k0 + kw],
                                       start=True, stop=not last)
                    mm = pe.matmul(w[:, at + width - P:at + width], ident16[:, :], future[:, :],
                                   start=False, stop=True)
                fill_done(mm, name)

            def max_turn(b, n):
                name = ("ms", b, n, 0)
                pe.wait_ge(max_split, b * NQ + n + 1)
                w = claim(name)
                mm = pe.transpose(w.bitcast(BF16)[0:3 * QUAD * NT, 0:P],
                                  max_parts[:, :, :].rearrange("p a n -> p (a n)"), ident16[:, :])
                fill_done(mm, name)

            def scores_unit(b, n, u):
                g, heads = UNITS[u]
                _, pieces, per = GROUPS[g]
                cnt = unit_count(b, n, u)
                if u == 0:
                    pe.wait_ge(shift_in, 48 * (b * NQ + n + 1))
                if cnt >= 3:
                    pe.wait_ge(exp_done, cnt - 2)
                bank = scores_bank(cnt)
                s = n % STACKS
                for j, h in enumerate(heads):
                    for kb, q0, w, at in pieces:
                        at += j * 2 * P
                        mm = pe.matmul(bank[:, at:at + w], k_stack[:, s, h, P * kb:P * (kb + 1)],
                                       q_stack[:, s, h, q0:q0 + w], start=True, stop=True)
                mm.then_inc(scores_ready, 1)

            def values(b, n, g):
                c, pieces, per = GROUPS[g]
                pe.wait_ge(exp_done, unit_count(b, n, GROUP_END[g] + 1))
                if is_diag(g):
                    pe.wait_ge(masked, b * NQ * NDIAG + diag_count(n, g))
                first, last = pieces[0][0] == 0, g == HALF_END[c]
                half_no = 2 * (b * NQ + n) + c
                if first and half_no:
                    pe.wait_ge(o_ready, half_no)
                buf = probs[:, ((b * NQ + n) * NG + g) % PGROUPS, :]
                for kb, q0, w, at in pieces:
                    for h in range(QUAD):
                        a = h * (HALF // per) + at
                        mm = pe.matmul(pv[32 * h:32 * (h + 1), q0 - HALF * c:q0 - HALF * c + w],
                                       v_aug[:, kb, QUAD * n + h, :], buf[:, a:a + w],
                                       start=first, stop=last)
                mm.then_inc(pv_done, 1)

            def turn_o(b, n, c):
                name = ("o", b, n, c)
                k = 2 * (b * NQ + n) + c
                pe.wait_ge(o_ready, k + 1)
                w = claim(name)
                for t in range(4):
                    mm = pe.transpose(w[:, P * t:P * (t + 1)], o_cols[:, k % 2, P * t:P * (t + 1)], ident[:, :])
                fill_done(mm, name)

            pe.wait_ge(consts_ready, 1)
            w = claim(("wsum", 0, 0, 0))
            pe.wait_ge(wide_ready, 1)
            fill_done(pe.matmul(w[:, 0:2], ones[:, :], wstat[:, 0:2], start=True, stop=True), ("wsum", 0, 0, 0))
            w = claim(("c2", 0, 0, 0))
            pe.wait_ge(wq_ready, 1)
            for c in range(HID // P):
                mm = pe.matmul(w[:, 0:C], lnb_wide[:, c, :], woutq[:, c, :], start=c == 0, stop=c == HID // P - 1)
            fill_done(mm, ("c2", 0, 0, 0))
            pe.wait_ge(ident_ready, 3)
            pe.wait_ge(weights_in, 160)

            for b in range(B):
                pe.wait_ge(xn_ready, b + 1)
                turn_tiles(("xT", b, 0, 0), xn)
                emptied(pe, ("xT", b, 0, 0))
                project(("lat", b, 0, 0), wlat[:, :], xnT)
                emptied(pe, ("lat", b, 0, 0))
                project(("q", b, 0, 0), wheads[:, 0, :], latT[0:3 * LAT])
                project(("k", b, 0, 0), wheads[:, 1, :], latT[0:3 * LAT])
                w = claim(("v", b, 0, 0))
                for t in range(NT):
                    mm = pe.matmul(w[:, P * t:P * (t + 1)], latT[0:3 * LAT, P * t:P * (t + 1)], wheads[:, 2, :],
                                   start=True, stop=True)
                fill_done(mm, ("v", b, 0, 0))

                for k in range(len(MAX_TILES)):
                    max_tile(b, 0, k)
                max_turn(b, 0)
                emptied(pe, ("v", b, 0, 0))
                for s in range(STEPS + TAIL):
                    if s < STEPS:
                        scores_unit(b, s // NU, s % NU)
                    for n, g in PV_AT.get(s, ()):
                        values(b, n, g)
                    for kind, n, k in TILES_AT.get(s, ()):
                        if kind == "max":
                            max_tile(b, n, k)
                        elif kind == "ms":
                            max_turn(b, n)
                        else:
                            turn_o(b, n, k)

                emptied(pe, ("o", b, NQ - 1, 0))
                emptied(pe, ("o", b, NQ - 1, 1))
                turn_tiles(("yT", b, 0, 0), y)
                emptied(pe, ("yT", b, 0, 0))
                w = claim(("proj", b, 0, 0))
                for t in range(NT):
                    mm = pe.matmul(w[:, P * t:P * (t + 1)], yT[:, P * t:P * (t + 1)], wproj[:, :],
                                   start=True, stop=True)
                fill_done(mm, ("proj", b, 0, 0))
                pe.wait_ge(x1n_ready, b + 1)
                turn_tiles(("x1T", b, 0, 0), x1n)
                emptied(pe, ("x1T", b, 0, 0))
                for k in range(4):
                    w = claim(("ffn1", b, 0, k))
                    for j in range(2):
                        t = 2 * k + j
                        mm = pe.matmul(w[:, HID * j:HID * (j + 1)], x1T[:, P * t:P * (t + 1)], wfcq[:, :],
                                       start=True, stop=True)
                    fill_done(mm, ("ffn1", b, 0, k))
                for k in range(4):
                    pe.wait_ge(gn_ready, 8 * b + 2 * k + 2)
                    w = claim(("hT", b, 0, k))
                    for j in range(8):
                        mm = pe.transpose(w[:, P * j:P * (j + 1)],
                                          gelu[:, 2 * k + j // 4, P * (j % 4):P * (j % 4 + 1)], ident[:, :])
                    fill_done(mm, ("hT", b, 0, k))
                w = claim(("ffn2", b, 0, 0))
                for t in range(NT):
                    if t % 2 == 0:
                        emptied(pe, ("hT", b, 0, t // 2))
                    for c in range(HID // P):
                        mm = pe.matmul(w[:, P * t:P * (t + 1)], gT[:, t, c, :], woutl[:, c, :],
                                       start=c == 0, stop=c == HID // P - 1)
                fill_done(mm, ("ffn2", b, 0, 0))

        @block.scalar
        def _(act):
            def copy_tile(dst, name, rows=P):
                filled(act, name)
                release(nc.scalar.copy(dst, work_flat(name)[0:rows, :]), name)

            def exponentials(b, n, u):
                g, _ = UNITS[u]
                cnt = unit_count(b, n, u)
                gno = (b * NQ + n) * NG + g
                act.wait_ge(scores_ready, cnt + 1)
                if gno >= PGROUPS:
                    act.wait_ge(pv_done, gno - PGROUPS + 1)
                first = GROUP_END[g - 1] + 1 if g else 0
                at = (u - first) * HALF
                nc.scalar.activation(probs[:, gno % PGROUPS, at:at + HALF], scores_bank(cnt), ACT.Exp,
                                     scale=SCALE).then_inc(exp_done, 1)

            def take_o(b, n, c):
                k = 2 * (b * NQ + n) + c
                act.wait_ge(pv_done, (b * NQ + n) * NG + HALF_END[c] + 1)
                if k >= 2:
                    filled(act, half_name(k - 2))
                nc.scalar.copy(o_cols[:, k % 2, :], pv).then_inc(o_ready, 1)

            for b in range(B):
                copy_tile(xnT[:, :], ("xT", b, 0, 0))
                copy_tile(latT[0:3 * LAT, :], ("lat", b, 0, 0), 3 * LAT)
                if b:
                    act.wait_ge(parts_out, 96 * b)
                for a, kind in enumerate("qk"):
                    filled(act, (kind, b, 0, 0))
                    nc.scalar.copy(parts[:, a, 0, :], work_flat((kind, b, 0, 0))).then_inc(part0_ready, 1)
                    emptied(act, (kind, b, 0, 0))
                    nc.scalar.copy(parts[:, a, 1, :], rest[:, a, :]).then_inc(part1_ready, 1)
                for s in range(STEPS + TAIL):
                    if s < STEPS:
                        exponentials(b, s // NU, s % NU)
                    if s in EVAC_AT:
                        take_o(b, *EVAC_AT[s])
                copy_tile(yT[:, :], ("yT", b, 0, 0))
                copy_tile(x1T[:, :], ("x1T", b, 0, 0))
                for k in range(4):
                    name = ("ffn1", b, 0, k)
                    filled(act, name)
                    release(nc.scalar.activation(gelu[:, 2 * k:2 * k + 2, :], work(name), ACT.Gelu), name)
                for k in range(4):
                    name = ("hT", b, 0, k)
                    filled(act, name)
                    release(nc.scalar.copy(gT[:, 2 * k:2 * k + 2].rearrange("p t c q -> p (t c q)"), work_flat(name)),
                            name)

        @block.vector
        def _(vec):
            chain = [0]

            def then_wait(ins):
                chain[0] += 1
                ins.then_inc(vec_done, 1)
                vec.wait_ge(vec_done, chain[0])

            def statistics(src, k, after=None):
                for t in range(NT):
                    if after:
                        after(t)
                    ins = nc.vector.bn_stats(stats[:, t, :], src[:, t, :])
                then_wait(ins)
                for t in range(NT):
                    ins = nc.vector.bn_aggr(mv[:, t, :], stats[:, t, :])
                then_wait(ins)
                nc.vector.tensor_scalar(veps[:, :], mv[:, :, 1], LN_EPS, None, ALU.add).then_inc(var_ready, 1)
                vec.wait_ge(rstd_ready, k + 1)

            def normalise(dst, src, t):
                return nc.vector.tensor_scalar(dst[:, t, :], src[:, t, :], mv[:, t, 0:1], rstd[:, t:t + 1],
                                               ALU.subtract, ALU.mult)

            def row_maxima(b, n, k):
                name = ("max", b, n, k)
                i, heads = MAX_TILES[k]
                width = P * (i + 1)
                filled(vec, name)
                w = work_flat(name)
                stride = max_place(i, 1) - max_place(i, 0)
                if len(heads) == 1:
                    src = w[:, 0:width]
                    dst = neg_max[:, heads[0], i:i + 1]
                else:
                    src = w[:, 0:stride * len(heads)].rearrange("p (h k) -> p h k", k=stride)[:, :, 0:width]
                    dst = neg_max[:, heads[0]:heads[-1] + 1, i]
                release(nc.vector.tensor_reduce(dst, src, AX.X, ALU.max, negate=True), name)

            def split_maxima(b, n):
                flat = neg_max[:, :, :].rearrange("p h i -> p (h i)")
                then_wait(nc.vector.tensor_copy(max_parts[:, 0, :], flat))
                then_wait(nc.vector.tensor_tensor(max_rest[:, :], flat, max_parts[:, 0, :], ALU.subtract))
                then_wait(nc.vector.tensor_copy(max_parts[:, 1, :], max_rest[:, :]))
                nc.vector.tensor_tensor(max_parts[:, 2, :], max_rest[:, :], max_parts[:, 1, :],
                                        ALU.subtract).then_inc(max_split, 1)

            def rows_of_maxima(b, n):
                name = ("ms", b, n, 0)
                filled(vec, name)
                if b * NQ + n:
                    vec.wait_ge(shift_in, 48 * (b * NQ + n))
                ins = nc.vector.tensor_copy(max_rows[:, :], work_flat(name).bitcast(BF16)[0:3 * QUAD * NT, 0:P])
                release(ins, name)

            def divide(b, n, c):
                name = ("o", b, n, c)
                filled(vec, name)
                w = work_flat(name)[:, 0:4 * P].rearrange("p (t h e) -> p t h e", t=4, h=QUAD)
                k = 2 * (b * NQ + n) + c
                if k:
                    emptied(vec, half_name(k - 1))
                then_wait(nc.vector.reciprocal(o_recip[:, :, :], w[:, :, :, HD]))
                dst = y[:, 4 * c:4 * c + 4, 32 * n:32 * (n + 1)].rearrange("p t (h d) -> p t h d", d=HD)
                ins = nc.vector.tensor_tensor(dst, w[:, :, :, 0:HD],
                                              o_recip[:, :, :].unsqueeze(3).to_broadcast([P, 4, QUAD, HD]), ALU.mult)
                release(ins, name)

            nc.vector.memset(ones[:, :], 1.0).then_inc(consts_ready, 1)
            vec.wait_ge(wsum_in, 32)
            nc.vector.tensor_reduce(wstat[:, 0:1], wfc[:, :], AX.X, ALU.add, apply_absolute_value=True)
            nc.vector.tensor_reduce(wstat[:, 1:2], wout[:, :, :].rearrange("p c d -> p (c d)"), AX.X, ALU.add,
                                    apply_absolute_value=True).then_inc(wide_ready, 1)
            then_wait(nc.vector.memset(k_stack[:, :, :, :].rearrange("r s h t -> r (s h t)").bitcast(U32), 0))
            nc.vector.memset(k_stack[SHIFT_ROW:SHIFT_ROW + 3].rearrange("r s h t -> r (s h t)"), 1.0
                             ).then_inc(stacks_set, 1)
            then_wait(nc.vector.memset(v_aug[:, :, :, :].rearrange("p t h e -> p (t h e)"), 0.0))
            then_wait(nc.vector.memset(v_aug[:, :, :, HD:HD + 1], 1.0))
            filled(vec, ("wsum", 0, 0, 0))
            ins = nc.vector.tensor_scalar(wstat[:, 2:4], work_flat(("wsum", 0, 0, 0))[:, 0:2], 1.0 / (HID * C),
                                          GAMMA_EPS, ALU.mult, ALU.add)
            release(ins, ("wsum", 0, 0, 0))
            vec.wait_ge(tile_free[TILE_NO[("wsum", 0, 0, 0)] % 2], 1)
            then_wait(nc.vector.reciprocal(wstat[:, 4:6], wstat[:, 2:4]))
            for j, (src, dst) in enumerate(((wfc[:, :], wfcq[:, :]),
                                            (wout[:, :, :].rearrange("p c d -> p (c d)"),
                                             woutq[:, :, :].rearrange("p c d -> p (c d)")))):
                nc.vector.tensor_scalar(dst, src, wstat[:, 4 + j:5 + j], 0.5, ALU.mult, ALU.is_gt)
                then_wait(nc.vector.tensor_scalar(wtmp[:, :], src, wstat[:, 4 + j:5 + j], -0.5, ALU.mult, ALU.is_lt))
                then_wait(nc.vector.tensor_tensor(dst, dst, wtmp[:, :], ALU.subtract))
            vec.wait_ge(weights_in, 160)
            for c in range(HID // P):
                nc.vector.tensor_scalar(woutl[:, c, :], woutq[:, c, :], lnw[:, c:c + 1], None, ALU.mult)
                ins = nc.vector.tensor_scalar(lnb_wide[:, c, :], ones[:, :], lnb[:, c:c + 1], None, ALU.mult)
            ins.then_inc(wq_ready, 1)
            filled(vec, ("c2", 0, 0, 0))
            release(nc.vector.tensor_copy(c2[:, :], work_flat(("c2", 0, 0, 0))[:, 0:C]), ("c2", 0, 0, 0))

            for b in range(B):
                vec.wait_ge(x_loaded, 16 * (b + 1))
                statistics(x_in[:, b], NORMS * b)
                for t in range(NT):
                    ins = normalise(xn, x_in[:, b], t)
                ins.then_inc(xn_ready, 1)
                for a, kind in enumerate("qk"):
                    name = (kind, b, 0, 0)
                    filled(vec, name)
                    vec.wait_ge(part0_ready, 2 * b + a + 1)
                    ins = nc.vector.tensor_tensor(rest[:, a, :], work_flat(name), parts[:, a, 0, :], ALU.subtract)
                    release(ins, name)
                name = ("v", b, 0, 0)
                filled(vec, name)
                ins = nc.vector.tensor_copy(v_aug[:, :, :, 0:HD],
                                            work_flat(name).rearrange("p (t h d) -> p t h d", t=NT, h=NH))
                release(ins, name)

                for k in range(len(MAX_TILES)):
                    row_maxima(b, 0, k)
                vec.wait_ge(tile_free[0], tile_frees(0, ("max", b, 0, len(MAX_TILES) - 1)))
                vec.wait_ge(tile_free[1], tile_frees(1, ("max", b, 0, len(MAX_TILES) - 1)))
                split_maxima(b, 0)
                rows_of_maxima(b, 0)
                for s in range(STEPS + TAIL):
                    for kind, n, k in TILES_AT.get(s, ()):
                        if kind == "max":
                            row_maxima(b, n, k)
                            if k == len(MAX_TILES) - 1:
                                vec.wait_ge(tile_free[0], tile_frees(0, ("max", b, n, k)))
                                vec.wait_ge(tile_free[1], tile_frees(1, ("max", b, n, k)))
                                split_maxima(b, n)
                        elif kind == "ms":
                            rows_of_maxima(b, n)
                        else:
                            divide(b, n, k)

                filled(vec, ("proj", b, 0, 0))
                if b:
                    vec.wait_ge(stored, 16 * b)
                ins = nc.vector.tensor_tensor(res[:, :, :], work_flat(("proj", b, 0, 0)).rearrange("p (t c) -> p t c", t=NT),
                                              bproj[:, :].unsqueeze(1).to_broadcast([P, NT, C]), ALU.add)
                release(ins, ("proj", b, 0, 0))
                vec.wait_ge(tile_free[TILE_NO[("proj", b, 0, 0)] % 2], TILE_NO[("proj", b, 0, 0)] // 2 + 1)
                statistics(res, NORMS * b + 1)
                for t in range(NT):
                    ins = normalise(res, res, t)
                then_wait(ins)
                then_wait(nc.vector.tensor_tensor(x1[:, :, :], res[:, :, :], x_in[:, b], ALU.add))
                statistics(x1, NORMS * b + 2)
                for t in range(NT):
                    ins = normalise(x1n, x1, t)
                ins.then_inc(x1n_ready, 1)
                statistics(gelu, NORMS * b + 3, lambda t: emptied(vec, ("ffn1", b, 0, t // 2)))
                for t in range(NT):
                    normalise(gelu, gelu, t).then_inc(gn_ready, 1)
                filled(vec, ("ffn2", b, 0, 0))
                ins = nc.vector.tensor_tensor(res[:, :, :], work_flat(("ffn2", b, 0, 0)).rearrange("p (t c) -> p t c", t=NT),
                                              c2[:, :].unsqueeze(1).to_broadcast([P, NT, C]), ALU.add)
                release(ins, ("ffn2", b, 0, 0))
                vec.wait_ge(tile_free[TILE_NO[("ffn2", b, 0, 0)] % 2], TILE_NO[("ffn2", b, 0, 0)] // 2 + 1)
                statistics(res, NORMS * b + 4)
                for t in range(NT):
                    ins = normalise(res, res, t)
                then_wait(ins)
                nc.vector.tensor_tensor(res[:, :, :], res[:, :, :], x1[:, :, :], ALU.add).then_inc(res_ready, 1)


def kernel(**inputs):
    import numpy as np
    import concourse.bacc as bacc
    from concourse.bass_utils import run_bass_kernel_spmd

    a = {k: np.asarray(v) for k, v in inputs.items()}
    arrays = {
        "x": a["L0_attn_x"],
        "wq_lat": a["L0_attn_wq_lat"], "wk_lat": a["L0_attn_wk_lat"], "wv_lat": a["L0_attn_wv_lat"],
        "wq_heads": a["L0_attn_wq_heads"], "wk_heads": a["L0_attn_wk_heads"], "wv_heads": a["L0_attn_wv_heads"],
        "w_proj": a["L0_attn_w_proj"], "b_proj": a["L0_attn_b_proj"],
        "w_fc_t": a["L0_ffn_W_fc"].T,
        "ln_w": a["L0_ffn_ln_w"].reshape(HID // P, P).T, "ln_b": a["L0_ffn_ln_b"].reshape(HID // P, P).T,
        "w_out_t": a["L0_ffn_W_proj"].T,
    }
    arrays = {k: np.ascontiguousarray(v) for k, v in arrays.items()}
    nc = bacc.Bacc("TRN2", target_bir_lowering=False, num_devices=1)
    ap = {k: nc.dram_tensor(f"in_{k}", v.shape, mybir.dt.from_np(v.dtype), kind="ExternalInput").ap()
          for k, v in arrays.items()}
    out = nc.dram_tensor("out", (B, T, C), F32, kind="ExternalOutput").ap()
    block_kernel(nc, ap["x"], (ap["wq_lat"], ap["wk_lat"], ap["wv_lat"]),
                 (ap["wq_heads"], ap["wk_heads"], ap["wv_heads"]), ap["w_proj"], ap["b_proj"],
                 ap["w_fc_t"], ap["ln_w"], ap["ln_b"], ap["w_out_t"], out)
    r = run_bass_kernel_spmd(nc, [{f"in_{k}": v for k, v in arrays.items()}], core_ids=[0])
    return r.results[0]["out"]
```

```python
from contextlib import ExitStack

import concourse.bass as bass
from concourse import mybir

ALU = mybir.AluOpType
ACT = mybir.ActivationFunctionType
AX = mybir.AxisListType
F32 = mybir.dt.float32
BF16 = mybir.dt.bfloat16
U32 = mybir.dt.uint32

P = 128
B, T, C = 2, 1024, 128
LAT = 32
NH, HD = 16, 8
HID = 512
NT = T // P
QUAD = 4
NQ = NH // QUAD
HALF = T // 2
HT = HALF // P
SCALE = HD ** -0.5
LN_EPS = 1e-5
GAMMA_EPS = 1e-6
MASKED = -3.0e38
ONES16 = 0x3F803F80
ROWS = 96
SHIFT_ROW = 64
STACKS = 3
PGROUPS = 4

Q_PARTS = (0, 0, 0, 1, 1, 2)
K_PARTS = (0, 1, 2, 0, 1, 0)
TERMS = len(Q_PARTS)
PART_ROWS = HD * TERMS

def score_groups():
    nb = HALF // P
    groups = []
    for c in range(2):
        for kb in range(nb * c):
            groups.append((c, [(kb, HALF * c, HALF, 0)], 1))
        d, e = nb * c, HALF * (c + 1)
        groups.append((c, [(d, P * d, HALF, 0)], 1))
        groups.append((c, [(d + 1, P * (d + 1), 3 * P, P), (d + 3, P * (d + 3), P, 0)], 1))
        groups.append((c, [(d + 2, P * (d + 2), 2 * P, 0)], 2))
    return groups


GROUPS = score_groups()
UNITS = [(g, tuple(range(i, i + GROUPS[g][2]))) for g in range(len(GROUPS)) for i in range(0, QUAD, GROUPS[g][2])]
NU = len(UNITS)
GROUP_END = [max(u for u, (g, _) in enumerate(UNITS) if g == j) for j in range(len(GROUPS))]
HALF_END = [max(j for j, x in enumerate(GROUPS) if x[0] == c) for c in range(2)]

MAX_TILES = [(0, (0, 1, 2, 3)), (1, (0, 1, 2, 3)), (2, (0, 1)), (2, (2, 3)), (3, (0, 1)), (3, (2, 3))]
MAX_TILES += [(i, (h,)) for i in range(4, NT) for h in range(QUAD)]

PV_LAG = 5
QUADS = B * NQ
STEPS = QUADS * NU
MAX_SPAN = 34
LEAD = 12
TAIL = 60

SPREAD = (0, 4, 7, 11, 15, 18, 21, 26, 26, 33, 35, 39, 43, 45, 49, 51, 55)
DENSE = (0, 1, 2, 4, 6, 7, 8, 9, 10, 11, 12, 13, 14, 15, 16, 17, 18)
AFTER = (("yT", 0), ("proj", 0), ("attn_pow", 0), ("attn_norm", 0), ("x1_pow", 0), ("x1_norm", 0), ("x1T", 0),
         ("ffn1", 0), ("ffn1", 1), ("g_stats", 0), ("g_pow", 0), ("g_norm", 0), ("hT", 0), ("hT", 1), ("ffn2", 0),
         ("out_pow", 0), ("out_norm", 0))


def schedule():
    at = {}

    def put(step, *event):
        at.setdefault(max(step, -1), []).append(event)

    def put_input(b, steps):
        for s, kind in zip(steps, ("ln1_stats", "ln1_pow", "ln1_norm", "xT", "lat", "q", "q_part1", "k", "k_part1",
                                   "v")):
            put(s, kind, b, 0, 0)

    put_input(0, (-1,) * 10)
    for n in range(QUADS):
        start = (n - 1) * NU - LEAD
        for k in range(len(MAX_TILES)):
            put(start + k * MAX_SPAN // len(MAX_TILES) if n else -1, "max", 0, n, k)
        put(start + MAX_SPAN if n else -1, "split", 0, n, 0)
        put(start + MAX_SPAN + 3 if n else -1, "ms", 0, n, 0)
        for g in range(len(GROUPS)):
            end = n * NU + GROUP_END[g]
            if is_diagonal(g):
                put(end, "mask", 0, n, g)
            put(end + PV_LAG, "values", 0, n, g)
        for c in range(2):
            done = n * NU + GROUP_END[HALF_END[c]] + PV_LAG
            put(done + 1, "take_o", 0, n, c)
            put(done + 4, "o", 0, n, c)
    put_input(1, (2, 4, 6, 10, 14, 18, 20, 22, 24, 28))
    for s, kind in ((44, "w_abs"), (46, "w_sum"), (50, "w_ternary"), (56, "c2")):
        put(s, kind, 0, 0, 0)
    for b in range(B):
        for h in range(2):
            ready = ((b + 1) * NQ - 1) * NU + GROUP_END[HALF_END[h]] + PV_LAG + 5
            steps = DENSE if b == B - 1 else SPREAD
            for s, (kind, k) in zip(steps, AFTER):
                put(ready + (40 if b < B - 1 and h else 0) + s, kind, b, h, k)
    return at


def is_diagonal(g):
    return any(P * kb == q0 for kb, q0, _, _ in GROUPS[g][1])


AT = schedule()
LAST = max(AT)

TILE_KINDS = ("xT", "lat", "q", "k", "v", "max", "ms", "o", "w_sum", "c2", "yT", "proj", "x1T", "ffn1", "hT", "ffn2")
TILE_NO = {e: i for i, e in enumerate(e for s in range(-1, LAST + 1) for e in AT.get(s, ()) if e[0] in TILE_KINDS)}
NORM_NO = {e[:3]: i for i, e in enumerate((e[0][:-4],) + e[1:] for s in range(-1, LAST + 1)
                                          for e in AT.get(s, ()) if e[0].endswith("_pow"))}


def max_place(i, j):
    return (P * (i + 1) if i < 2 else HALF) * j


def block_kernel(nc, x, w_lat, w_heads, w_proj, b_proj, w_fc_t, ln_w, ln_b, w_out_t, out):
    with ExitStack() as ctx:
        def sb(name, shape, dt=F32):
            return ctx.enter_context(nc.sbuf_tensor(name, shape, dt))

        def sem(name):
            return ctx.enter_context(nc.semaphore(name))

        ident = sb("ident", [P, P])
        ident16 = sb("ident16", [P, P], BF16)
        future = sb("future", [P, P], BF16)
        ones = sb("ones", [P, P])
        minus_half = sb("minus_half", [P, NT])
        wlat = sb("wlat", [P, 3 * LAT])
        wheads = sb("wheads", [3 * LAT, 3, C])
        wproj = sb("wproj", [C, C])
        bproj = sb("bproj", [P, C])
        wfc = sb("wfc", [P, HID])
        wfcq = sb("wfcq", [P, HID])
        wout = sb("wout", [P, HID // P, C])
        woutq = sb("woutq", [P, HID // P, C])
        woutl = sb("woutl", [P, HID // P, C])
        lnw = sb("lnw", [P, HID // P])
        lnb = sb("lnb", [P, HID // P])
        lnb_wide = sb("lnb_wide", [P, HID // P, P])
        c2 = sb("c2", [P, C])
        wstat = sb("wstat", [P, 8])
        wtmp = sb("wtmp", [P, HID])

        x_in = sb("x_in", [P, B, NT, C])
        xn = sb("xn", [P, NT, C])
        xnT = sb("xnT", [C, T])
        latT = sb("latT", [C, T])
        parts = sb("parts", [P, 2, 3, T], BF16)
        rest = sb("rest", [P, 2, T])
        v_aug = sb("v_aug", [P, B, NT, NH, HD + 1])
        q_stack = sb("q_stack", [ROWS, STACKS, QUAD, T], BF16)
        k_stack = sb("k_stack", [ROWS, STACKS, QUAD, T], BF16)
        neg_max = sb("neg_max", [P, QUAD, NT])
        max_rest = sb("max_rest", [P, QUAD * NT])
        max_parts = sb("max_parts", [P, 3, QUAD * NT], BF16)
        max_rows = sb("max_rows", [3 * QUAD * NT, P], BF16)
        probs = sb("probs", [P, PGROUPS, QUAD * HALF])
        o_cols = sb("o_cols", [P, 2, HALF])
        o_recip = sb("o_recip", [P, 4, QUAD])
        y = sb("y", [P, B, NT, C])
        yT = sb("yT", [C, HALF])
        x1 = sb("x1", [P, 2, HT, C])
        x1n = sb("x1n", [P, 2, HT, C])
        x1T = sb("x1T", [C, HALF])
        gelu = sb("gelu", [P, HT, HID])
        gn = sb("gn", [P, HT, HID])
        gT = sb("gT", [P, HT, HID // P, P])
        res = sb("res", [P, 2, HT, C])
        stats = sb("stats", [P, 4, NT, 6])
        mv = sb("mv", [P, 4, NT, 2])
        veps = sb("veps", [P, 4, NT])
        rstd = sb("rstd", [P, 4, NT])

        ps = ctx.enter_context(nc.psum_tensor("ps", [P, 8, 512], F32))
        pv = ps[:, 7]

        def work(name):
            return ps[:, 2 * (TILE_NO[name] % 2):2 * (TILE_NO[name] % 2) + 2, :]

        def work_flat(name):
            return work(name).rearrange("p a n -> p (a n)")

        def scores_bank(u):
            return ps[:, 4 + u % 3]

        image = nc.dram_tensor("image", [B, 2, NH, HD, TERMS, T], BF16, kind="Internal").ap()

        weights_in = sem("weights_in")
        ternary_in = sem("ternary_in")
        x_in0, x_in1 = sem("x_in0"), sem("x_in1")
        pads_zeroed = sem("pads_zeroed")
        stacks_set = sem("stacks_set")
        ident_ready = sem("ident_ready")
        ones_ready = sem("ones_ready")
        v_ones = sem("v_ones")
        bank_zeroed = sem("bank_zeroed")
        vec_done = sem("vec_done")
        pool_done = sem("pool_done")
        act_done = sem("act_done")
        tile_ready = [sem("tile_ready0"), sem("tile_ready1")]
        tile_free = [sem("tile_free0"), sem("tile_free1")]
        w_abs_ready = sem("w_abs_ready")
        ternary_ready = sem("ternary_ready")
        var_ready = sem("var_ready")
        rstd_ready = sem("rstd_ready")
        xn_ready = sem("xn_ready")
        part0_ready = sem("part0_ready")
        part1_ready = sem("part1_ready")
        part2_ready = sem("part2_ready")
        image_out = sem("image_out")
        stack_in = [sem(f"stack_in{i}") for i in range(STACKS)]
        max_split = sem("max_split")
        shift_in = sem("shift_in")
        scores_ready = sem("scores_ready")
        exp_done = sem("exp_done")
        masked = sem("masked")
        pv_done = sem("pv_done")
        o_ready = sem("o_ready")
        x1n_ready = sem("x1n_ready")
        gn_ready = sem("gn_ready")
        res_ready = sem("res_ready")
        stored = [sem("stored0"), sem("stored1")]

        NG = len(GROUPS)
        DIAGONALS = [g for g in range(NG) if is_diagonal(g)]

        def filled(eng, name):
            i = TILE_NO[name]
            eng.wait_ge(tile_ready[i % 2], i // 2 + 1)

        def emptied(eng, name):
            i = TILE_NO[name]
            eng.wait_ge(tile_free[i % 2], i // 2 + 1)

        def release(ins, name):
            ins.then_inc(tile_free[TILE_NO[name] % 2], 1)

        def bank_no(n, u):
            return n * NU + u

        def half_name(k):
            return "o", 0, k // 2, k % 2

        def norm_slot(*which):
            return NORM_NO[which] % 4

        block = ctx.enter_context(nc.Block())

        @block.sync
        def _(sp):
            for b, arrived in enumerate((x_in0, x_in1)):
                sp.dma_start(x_in[:, b], x[b].rearrange("(t p) c -> p t c", p=P)).then_inc(arrived, 16)
            for i in range(3):
                sp.dma_start(wlat[:, LAT * i:LAT * (i + 1)], w_lat[i]).then_inc(weights_in, 16)
            sp.wait_ge(pads_zeroed, 1)
            for i in range(3):
                sp.dma_start(wheads[LAT * i:LAT * (i + 1), i, :], w_heads[i]).then_inc(weights_in, 16)
            sp.dma_start(wfc[:, :], w_fc_t).then_inc(ternary_in, 16)
            sp.dma_start(wout[:, :, :], w_out_t.rearrange("(c p) d -> p c d", p=P)).then_inc(ternary_in, 16)
            sp.dma_start(lnw[:, :], ln_w).then_inc(ternary_in, 16)
            sp.dma_start(lnb[:, :], ln_b).then_inc(ternary_in, 16)
            sp.dma_start(wproj[:, :], w_proj).then_inc(ternary_in, 16)
            sp.dma_start(bproj[:, :], b_proj.rearrange("(a c) -> a c", a=1).to_broadcast([P, C])
                         ).then_inc(ternary_in, 16)

            def store_image(b):
                for r, ready in ((0, part0_ready), (1, part1_ready), (2, part2_ready)):
                    sp.wait_ge(ready, 2 * b + 1)
                    for i in [i for i in range(TERMS) if Q_PARTS[i] == r]:
                        sp.dma_start(image[b, 0, :, :, i, :], parts[:, 0, r, :]).then_inc(image_out, 16)
                sp.wait_ge(part2_ready, 2 * b + 2)
                for i in [i for i in range(TERMS) if K_PARTS[i] == 0]:
                    m = len([j for j in range(i, TERMS) if K_PARTS[j] == j - i])
                    sp.dma_start(image[b, 1, :, :, i:i + m, :], parts[:, 1, 0:m, :]).then_inc(image_out, 16)
                sp.wait_ge(image_out, 16 * 9 * (b + 1))

            def load_stacks(n):
                s = n % STACKS
                b, heads = n // NQ, slice(QUAD * (n % NQ), QUAD * (n % NQ + 1))
                if n >= STACKS:
                    sp.wait_ge(scores_ready, bank_no(n - STACKS + 1, 0))
                for a, stack in enumerate((q_stack, k_stack)):
                    sp.dma_start(stack[0:PART_ROWS, s], image[b, a, heads].rearrange("h d r t -> (d r) h t")
                                 ).then_inc(stack_in[s], 16)
                sp.dma_start(q_stack[SHIFT_ROW:SHIFT_ROW + 3, s], k_stack[PART_ROWS:PART_ROWS + 3, s]
                             ).then_inc(stack_in[s], 16)

            def store_shift(n):
                emptied(sp, ("ms", 0, n, 0))
                sp.dma_start(q_stack[SHIFT_ROW:SHIFT_ROW + 3, n % STACKS].rearrange("a h (i q) -> a (h i) q", q=P),
                             max_rows[:, :]).then_inc(shift_in, 16)

            store_image(0)
            sp.wait_ge(stacks_set, 3)
            load_stacks(0)
            load_stacks(1)
            for n in range(QUADS):
                store_shift(n)
                if n == 1:
                    store_image(1)
                if n + 2 < QUADS:
                    load_stacks(n + 2)
            for k in range(2 * B):
                sp.wait_ge(res_ready, k + 1)
                sp.dma_start(out[k // 2].rearrange("(t p) c -> p t c", p=P)[:, HT * (k % 2):HT * (k % 2 + 1)],
                             res[:, k % 2]).then_inc(stored[k % 2], 16)
            for half in stored:
                sp.wait_ge(half, 16 * B)

        @block.gpsimd
        def _(pool):
            nc.gpsimd.memset(wheads[:, :, :], 0.0).then_inc(pads_zeroed, 1)
            nc.gpsimd.memset(minus_half[:, :], -0.5)
            nc.gpsimd.memset(ident[:, :], 0.0)
            nc.gpsimd.memset(ident16[:, :], 0.0)
            nc.gpsimd.memset(future[:, :], 0.0).then_inc(pool_done, 1)
            pool.wait_ge(pool_done, 1)
            for t in (ident, ident16):
                nc.gpsimd.affine_select(out=t[:, :], in_=t[:, :], compare_op=ALU.not_equal, fill=1.0, base=0,
                                        pattern=[[-1, P]], channel_multiplier=1).then_inc(ident_ready, 1)
            nc.gpsimd.affine_select(out=future[:, :], in_=future[:, :], compare_op=ALU.is_ge, fill=MASKED, base=0,
                                    pattern=[[-1, P]], channel_multiplier=1).then_inc(ident_ready, 1)

            def inverse_std(which):
                k, m = NORM_NO[which], NT if which[0] == "ln1" else HT
                pool.wait_ge(var_ready, k + 1)
                nc.gpsimd.tensor_tensor(rstd[:, k % 4, 0:m], veps[:, k % 4, 0:m], minus_half[:, 0:m], ALU.pow
                                        ).then_inc(rstd_ready, 1)

            def last_part(b, a):
                pool.wait_ge(part1_ready, 2 * b + a + 1)
                nc.gpsimd.tensor_tensor(parts[:, a, 2, :], rest[:, a, :], parts[:, a, 1, :],
                                        ALU.subtract).then_inc(part2_ready, 1)

            def mask(n, g):
                _, pieces, per = GROUPS[g]
                pool.wait_ge(exp_done, bank_no(n, GROUP_END[g] + 1))
                buf = probs[:, (n * NG + g) % PGROUPS, :]
                share = HALF // per
                v = buf[:, 0:QUAD * share].rearrange("p (h q) -> p h q", h=QUAD)[:, :, 0:len(pieces) * P]
                nc.gpsimd.affine_select(out=v, in_=v, compare_op=ALU.is_ge, fill=0.0, base=0,
                                        pattern=[[0, QUAD], [0, len(pieces)], [1, P]][:: 1 if len(pieces) > 1 else 2],
                                        channel_multiplier=-1).then_inc(masked, 1)

            for s in range(-1, LAST + 1):
                for kind, b, n, k in AT.get(s, ()):
                    if kind.endswith("_pow"):
                        inverse_std((kind[:-4], b, n))
                    elif kind == "q_part1":
                        last_part(b, 0)
                        if b == 0:
                            nc.gpsimd.memset(q_stack[:, :, :, :].rearrange("r s h t -> r (s h t)").bitcast(U32), 0
                                             ).then_inc(stacks_set, 1)
                    elif kind == "k_part1":
                        last_part(b, 1)
                    elif kind == "mask":
                        mask(n, k)

        @block.tensor
        def _(pe):
            def claim(name):
                i = TILE_NO[name]
                if i >= 2:
                    pe.wait_ge(tile_free[i % 2], i // 2)
                return work_flat(name)

            def fill_done(ins, name):
                ins.then_inc(tile_ready[TILE_NO[name] % 2], 1)

            def turn_tiles(name, tiles):
                w = claim(name)
                for t, src in enumerate(tiles):
                    mm = pe.transpose(w[:, P * t:P * (t + 1)], src, ident[:, :])
                fill_done(mm, name)

            def project(name, lhs, rhs):
                w = claim(name)
                for c in range(2):
                    mm = pe.matmul(w[0:lhs.shape[1], HALF * c:HALF * (c + 1)], lhs, rhs[:, HALF * c:HALF * (c + 1)],
                                   start=True, stop=True)
                fill_done(mm, name)

            def by_token(name, lhsT, rhs, tiles):
                w = claim(name)
                m = rhs.shape[1]
                for i, t in enumerate(tiles):
                    mm = pe.matmul(w[:, m * i:m * (i + 1)], lhsT[:, P * t:P * (t + 1)], rhs, start=True, stop=True)
                fill_done(mm, name)

            def max_tile(n, k):
                name = ("max", 0, n, k)
                i, heads = MAX_TILES[k]
                s = n % STACKS
                if k == 0:
                    pe.wait_ge(stack_in[s], 48 * (n // STACKS + 1))
                w = claim(name)
                width = P * (i + 1)
                for j, h in enumerate(heads):
                    at = max_place(i, j)
                    lhs = q_stack[:, s, h, P * i:P * (i + 1)]
                    for k0 in range(0, width, 512):
                        kw = min(512, width - k0)
                        mm = pe.matmul(w[:, at + k0:at + k0 + kw], lhs, k_stack[:, s, h, k0:k0 + kw],
                                       start=True, stop=k0 + kw != width)
                    mm = pe.matmul(w[:, at + width - P:at + width], ident16[:, :], future[:, :],
                                   start=False, stop=True)
                fill_done(mm, name)

            def max_turn(n):
                name = ("ms", 0, n, 0)
                pe.wait_ge(max_split, n + 1)
                w = claim(name)
                mm = pe.transpose(w.bitcast(BF16)[0:3 * QUAD * NT, 0:P],
                                  max_parts[:, :, :].rearrange("p a n -> p (a n)"), ident16[:, :])
                fill_done(mm, name)

            def scores_unit(n, u):
                g, heads = UNITS[u]
                cnt = bank_no(n, u)
                if u == 0:
                    pe.wait_ge(shift_in, 16 * (n + 1))
                if cnt >= 3:
                    pe.wait_ge(exp_done, cnt - 2)
                bank = scores_bank(cnt)
                s = n % STACKS
                for j, h in enumerate(heads):
                    for kb, q0, w, at in GROUPS[g][1]:
                        at += j * (HALF // len(heads))
                        mm = pe.matmul(bank[:, at:at + w], k_stack[:, s, h, P * kb:P * (kb + 1)],
                                       q_stack[:, s, h, q0:q0 + w], start=True, stop=True)
                mm.then_inc(scores_ready, 1)

            def values(n, g):
                c, pieces, per = GROUPS[g]
                pe.wait_ge(exp_done, bank_no(n, GROUP_END[g] + 1))
                if g in DIAGONALS:
                    pe.wait_ge(masked, n * len(DIAGONALS) + DIAGONALS.index(g) + 1)
                if n % NQ == 0 and g == 0:
                    emptied(pe, ("v", n // NQ, 0, 0))
                first, last = pieces[0][0] == 0, g == HALF_END[c]
                if first and 2 * n + c:
                    pe.wait_ge(o_ready, 2 * n + c)
                buf = probs[:, (n * NG + g) % PGROUPS, :]
                for kb, q0, w, at in pieces:
                    for h in range(QUAD):
                        a = h * (HALF // per) + at
                        mm = pe.matmul(pv[32 * h:32 * h + HD + 1, q0 - HALF * c:q0 - HALF * c + w],
                                       v_aug[:, n // NQ, kb, QUAD * (n % NQ) + h, :], buf[:, a:a + w],
                                       start=first, stop=last)
                mm.then_inc(pv_done, 1)

            def turn_o(n, c):
                k = 2 * n + c
                pe.wait_ge(o_ready, k + 1)
                turn_tiles(("o", 0, n, c), [o_cols[:, k % 2, P * t:P * (t + 1)] for t in range(HT)])

            pe.wait_ge(bank_zeroed, 1)
            pe.wait_ge(ident_ready, 3)
            pe.wait_ge(v_ones, 1)
            for s in range(-1, LAST + 1):
                if 0 <= s < STEPS:
                    scores_unit(s // NU, s % NU)
                for kind, b, n, k in AT.get(s, ()):
                    name = (kind, b, n, k)
                    if kind == "max":
                        max_tile(n, k)
                    elif kind == "ms":
                        max_turn(n)
                    elif kind == "values":
                        values(n, k)
                    elif kind == "o":
                        turn_o(n, k)
                    elif kind == "xT":
                        pe.wait_ge(xn_ready, b + 1)
                        turn_tiles(name, [xn[:, t, :] for t in range(NT)])
                    elif kind == "lat":
                        if b == 0:
                            pe.wait_ge(weights_in, 96)
                        emptied(pe, ("xT", b, 0, 0))
                        project(name, wlat[:, :], xnT)
                    elif kind in ("q", "k"):
                        emptied(pe, ("lat", b, 0, 0))
                        project(name, wheads[:, "qk".index(kind), :], latT[0:3 * LAT])
                    elif kind == "v":
                        by_token(name, latT[0:3 * LAT], wheads[:, 2, :], range(NT))
                    elif kind == "w_sum":
                        pe.wait_ge(w_abs_ready, 1)
                        w = claim(name)
                        fill_done(pe.matmul(w[:, 0:2], ones[:, :], wstat[:, 0:2], start=True, stop=True), name)
                    elif kind == "c2":
                        pe.wait_ge(ternary_ready, 1)
                        w = claim(name)
                        for c in range(HID // P):
                            mm = pe.matmul(w[:, 0:C], lnb_wide[:, c, :], woutq[:, c, :], start=c == 0,
                                           stop=c == HID // P - 1)
                        fill_done(mm, name)
                    elif kind == "yT":
                        emptied(pe, ("o", 0, NQ * (b + 1) - 1, n))
                        turn_tiles(name, [y[:, b, HT * n + t, :] for t in range(HT)])
                    elif kind == "proj":
                        emptied(pe, ("yT", b, n, 0))
                        by_token(name, yT, wproj[:, :], range(HT))
                    elif kind == "x1T":
                        pe.wait_ge(x1n_ready, 2 * b + n + 1)
                        turn_tiles(name, [x1n[:, n, t, :] for t in range(HT)])
                    elif kind == "ffn1":
                        emptied(pe, ("x1T", b, n, 0))
                        by_token(name, x1T, wfcq[:, :], (2 * k, 2 * k + 1))
                    elif kind == "hT":
                        pe.wait_ge(gn_ready, HT * (2 * b + n) + 2 * k + 2)
                        turn_tiles(name, [gn[:, 2 * k + j // 4, P * (j % 4):P * (j % 4 + 1)] for j in range(8)])
                    elif kind == "ffn2":
                        w = claim(name)
                        for t in range(HT):
                            if t % 2 == 0:
                                emptied(pe, ("hT", b, n, t // 2))
                            for c in range(HID // P):
                                mm = pe.matmul(w[:, P * t:P * (t + 1)], gT[:, t, c, :], woutl[:, c, :],
                                               start=c == 0, stop=c == HID // P - 1)
                        fill_done(mm, name)

        @block.scalar
        def _(act):
            steps_done = [0]

            def then_wait(ins):
                steps_done[0] += 1
                ins.then_inc(act_done, 1)
                act.wait_ge(act_done, steps_done[0])

            def exponentials(n, u):
                g, _ = UNITS[u]
                cnt, group = bank_no(n, u), n * NG + g
                act.wait_ge(scores_ready, cnt + 1)
                if group >= PGROUPS:
                    act.wait_ge(pv_done, group - PGROUPS + 1)
                at = (u - (GROUP_END[g - 1] + 1 if g else 0)) * HALF
                nc.scalar.activation(probs[:, group % PGROUPS, at:at + HALF], scores_bank(cnt), ACT.Exp,
                                     scale=SCALE).then_inc(exp_done, 1)

            def take_o(n, c):
                k = 2 * n + c
                act.wait_ge(pv_done, n * NG + HALF_END[c] + 1)
                if k >= 2:
                    filled(act, half_name(k - 2))
                nc.scalar.copy(o_cols[:, k % 2, :], pv).then_inc(o_ready, 1)

            def copy_tile(dst, name, rows=P):
                filled(act, name)
                src = work_flat(name)[0:rows, 0:dst.free_size()]
                release(nc.scalar.copy(dst, src), name)

            for s in range(-1, LAST + 1):
                if 0 <= s < STEPS:
                    exponentials(s // NU, s % NU)
                for kind, b, n, k in AT.get(s, ()):
                    name = (kind, b, n, k)
                    if kind == "take_o":
                        take_o(n, k)
                    elif kind == "xT":
                        copy_tile(xnT[:, :], name)
                    elif kind == "lat":
                        copy_tile(latT[0:3 * LAT, :], name, 3 * LAT)
                    elif kind in ("q", "k"):
                        if b and kind == "q":
                            act.wait_ge(image_out, 144 * b)
                        filled(act, name)
                        nc.scalar.copy(parts[:, "qk".index(kind), 0, :], work_flat(name)).then_inc(part0_ready, 1)
                    elif kind in ("q_part1", "k_part1"):
                        a = "qk".index(kind[0])
                        emptied(act, (kind[0], b, 0, 0))
                        nc.scalar.copy(parts[:, a, 1, :], rest[:, a, :]).then_inc(part1_ready, 1)
                    elif kind == "v":
                        filled(act, name)
                        release(nc.scalar.copy(v_aug[:, b, :, :, 0:HD],
                                               work_flat(name).rearrange("p (t h d) -> p t h d", t=NT, h=NH)), name)
                    elif kind == "yT":
                        copy_tile(yT[:, :], name)
                    elif kind == "x1T":
                        copy_tile(x1T[:, :], name)
                    elif kind == "ffn1":
                        filled(act, name)
                        release(nc.scalar.activation(gelu[:, 2 * k:2 * k + 2, :], work(name), ACT.Gelu), name)
                    elif kind == "hT":
                        copy_tile(gT[:, 2 * k:2 * k + 2].rearrange("p t c q -> p (t c q)"), name)

        @block.vector
        def _(vec):
            steps_done = [0]

            def then_wait(ins):
                steps_done[0] += 1
                ins.then_inc(vec_done, 1)
                vec.wait_ge(vec_done, steps_done[0])

            def statistics(which, tiles):
                k = NORM_NO[which] % 4
                for t, src in enumerate(tiles):
                    ins = nc.vector.bn_stats(stats[:, k, t, :], src)
                then_wait(ins)
                for t in range(len(tiles)):
                    ins = nc.vector.bn_aggr(mv[:, k, t, :], stats[:, k, t, :])
                then_wait(ins)
                nc.vector.tensor_scalar(veps[:, k, 0:len(tiles)], mv[:, k, 0:len(tiles), 1], LN_EPS, None, ALU.add
                                        ).then_inc(var_ready, 1)

            def normalise(which, dst, src):
                k = NORM_NO[which]
                vec.wait_ge(rstd_ready, k + 1)
                for t in range(len(src)):
                    ins = nc.vector.tensor_scalar(dst[t], src[t], mv[:, k % 4, t, 0:1], rstd[:, k % 4, t:t + 1],
                                                  ALU.subtract, ALU.mult)
                return ins

            def row_maxima(n, k):
                name = ("max", 0, n, k)
                i, heads = MAX_TILES[k]
                width = P * (i + 1)
                filled(vec, name)
                w = work_flat(name)
                if len(heads) == 1:
                    src, dst = w[:, 0:width], neg_max[:, heads[0], i:i + 1]
                else:
                    stride = max_place(i, 1)
                    src = w[:, 0:stride * len(heads)].rearrange("p (h k) -> p h k", k=stride)[:, :, 0:width]
                    dst = neg_max[:, heads[0]:heads[-1] + 1, i]
                release(nc.vector.tensor_reduce(dst, src, AX.X, ALU.max, negate=True), name)

            def split_maxima(n):
                for k in (len(MAX_TILES) - 2, len(MAX_TILES) - 1):
                    emptied(vec, ("max", 0, n, k))
                flat = neg_max[:, :, :].rearrange("p h i -> p (h i)")
                then_wait(nc.vector.tensor_copy(max_parts[:, 0, :], flat))
                then_wait(nc.vector.tensor_tensor(max_rest[:, :], flat, max_parts[:, 0, :], ALU.subtract))
                then_wait(nc.vector.tensor_copy(max_parts[:, 1, :], max_rest[:, :]))
                nc.vector.tensor_tensor(max_parts[:, 2, :], max_rest[:, :], max_parts[:, 1, :],
                                        ALU.subtract).then_inc(max_split, 1)

            def rows_of_maxima(n):
                name = ("ms", 0, n, 0)
                filled(vec, name)
                if n:
                    vec.wait_ge(shift_in, 16 * n)
                release(nc.vector.tensor_copy(max_rows[:, :], work_flat(name).bitcast(BF16)[0:3 * QUAD * NT, 0:P]),
                        name)

            def divide(n, c):
                name = ("o", 0, n, c)
                filled(vec, name)
                w = work_flat(name)[:, 0:HT * P].rearrange("p (t h e) -> p t h e", t=HT, h=QUAD)
                if 2 * n + c:
                    emptied(vec, half_name(2 * n + c - 1))
                then_wait(nc.vector.reciprocal(o_recip[:, :, :], w[:, :, :, HD]))
                m = QUAD * HD
                dst = y[:, n // NQ, HT * c:HT * (c + 1), m * (n % NQ):m * (n % NQ + 1)].rearrange("p t (h d) -> p t h d", d=HD)
                release(nc.vector.tensor_tensor(dst, w[:, :, :, 0:HD],
                                                o_recip[:, :, :].unsqueeze(3).to_broadcast([P, HT, QUAD, HD]),
                                                ALU.mult), name)

            def add_bias(name, dst, bias):
                filled(vec, name)
                release(nc.vector.tensor_tensor(dst, work_flat(name)[:, 0:HALF].rearrange("p (t c) -> p t c", t=HT),
                                                bias.unsqueeze(1).to_broadcast([P, HT, C]), ALU.add), name)
                emptied(vec, name)

            def tiles_of(half):
                return [half[:, t, :] for t in range(HT)]

            wout_flat = wout[:, :, :].rearrange("p c d -> p (c d)")
            woutq_flat = woutq[:, :, :].rearrange("p c d -> p (c d)")

            nc.vector.memset(pv, 0.0).then_inc(bank_zeroed, 1)
            nc.vector.memset(v_aug[:, :, :, :, HD:HD + 1].rearrange("p b t h e -> p (b t h) e"), 1.0
                             ).then_inc(v_ones, 1)
            for s in range(-1, LAST + 1):
                for kind, b, n, k in AT.get(s, ()):
                    name = (kind, b, n, k)
                    if kind == "max":
                        row_maxima(n, k)
                    elif kind == "split":
                        split_maxima(n)
                    elif kind == "ms":
                        rows_of_maxima(n)
                    elif kind == "o":
                        divide(n, k)
                    elif kind == "ln1_stats":
                        vec.wait_ge(x_in1 if b else x_in0, 16)
                        statistics(("ln1", b, 0), [x_in[:, b, t, :] for t in range(NT)])
                        if b == 0:
                            nc.vector.memset(ones[:, :], 1.0).then_inc(ones_ready, 1)
                            then_wait(nc.vector.memset(
                                k_stack[:, :, :, :].rearrange("r s h t -> r (s h t)").bitcast(U32), 0))
                    elif kind == "ln1_norm":
                        normalise(("ln1", b, 0), [xn[:, t, :] for t in range(NT)],
                                  [x_in[:, b, t, :] for t in range(NT)]).then_inc(xn_ready, 1)
                        if b == 0:
                            nc.vector.memset(k_stack[SHIFT_ROW:SHIFT_ROW + 3].rearrange("r s h t -> r (s h t)")
                                             .bitcast(U32), ONES16).then_inc(stacks_set, 2)
                    elif kind in ("q", "k"):
                        a = "qk".index(kind)
                        filled(vec, name)
                        vec.wait_ge(part0_ready, 2 * b + a + 1)
                        release(nc.vector.tensor_tensor(rest[:, a, :], work_flat(name), parts[:, a, 0, :],
                                                        ALU.subtract), name)
                    elif kind == "w_abs":
                        vec.wait_ge(ternary_in, 96)
                        nc.vector.tensor_reduce(wstat[:, 0:1], wfc[:, :], AX.X, ALU.add, apply_absolute_value=True)
                        nc.vector.tensor_reduce(wstat[:, 1:2], wout_flat, AX.X, ALU.add,
                                                apply_absolute_value=True).then_inc(w_abs_ready, 1)
                    elif kind == "w_sum":
                        filled(vec, name)
                        release(nc.vector.tensor_scalar(wstat[:, 2:4], work_flat(name)[:, 0:2], 1.0 / (HID * C),
                                                        GAMMA_EPS, ALU.mult, ALU.add), name)
                        emptied(vec, name)
                        then_wait(nc.vector.reciprocal(wstat[:, 4:6], wstat[:, 2:4]))
                    elif kind == "w_ternary":
                        for j, (src, dst) in enumerate(((wfc[:, :], wfcq[:, :]), (wout_flat, woutq_flat))):
                            gamma = wstat[:, 4 + j:5 + j]
                            nc.vector.tensor_scalar(dst, src, gamma, 0.5, ALU.mult, ALU.is_gt)
                            then_wait(nc.vector.tensor_scalar(wtmp[:, :], src, gamma, -0.5, ALU.mult, ALU.is_lt))
                            then_wait(nc.vector.tensor_tensor(dst, dst, wtmp[:, :], ALU.subtract))
                        for c in range(HID // P):
                            nc.vector.tensor_scalar(woutl[:, c, :], woutq[:, c, :], lnw[:, c:c + 1], None, ALU.mult)
                            ins = nc.vector.tensor_scalar(lnb_wide[:, c, :], ones[:, :], lnb[:, c:c + 1], None,
                                                          ALU.mult)
                        ins.then_inc(ternary_ready, 1)
                    elif kind == "c2":
                        filled(vec, name)
                        release(nc.vector.tensor_copy(c2[:, :], work_flat(name)[:, 0:C]), name)
                    elif kind == "proj":
                        if b:
                            vec.wait_ge(stored[n], 16)
                        add_bias(name, res[:, n], bproj[:, :])
                        statistics(("attn", b, n), tiles_of(res[:, n]))
                    elif kind == "attn_norm":
                        then_wait(normalise(("attn", b, n), tiles_of(res[:, n]), tiles_of(res[:, n])))
                        then_wait(nc.vector.tensor_tensor(x1[:, n], res[:, n], x_in[:, b, HT * n:HT * (n + 1)],
                                                          ALU.add))
                        statistics(("x1", b, n), tiles_of(x1[:, n]))
                    elif kind == "x1_norm":
                        normalise(("x1", b, n), tiles_of(x1n[:, n]), tiles_of(x1[:, n])).then_inc(x1n_ready, 1)
                    elif kind == "g_stats":
                        for j in range(2):
                            emptied(vec, ("ffn1", b, n, j))
                        statistics(("g", b, n), tiles_of(gelu))
                    elif kind == "g_norm":
                        m = NORM_NO["g", b, n]
                        vec.wait_ge(rstd_ready, m + 1)
                        if 2 * b + n:
                            filled(vec, ("hT", (2 * b + n - 1) // 2, (n + 1) % 2, 1))
                        for t in range(HT):
                            nc.vector.tensor_scalar(gn[:, t, :], gelu[:, t, :], mv[:, m % 4, t, 0:1],
                                                    rstd[:, m % 4, t:t + 1], ALU.subtract, ALU.mult
                                                    ).then_inc(gn_ready, 1)
                    elif kind == "ffn2":
                        add_bias(name, res[:, n], c2[:, :])
                        statistics(("out", b, n), tiles_of(res[:, n]))
                    elif kind == "out_norm":
                        then_wait(normalise(("out", b, n), tiles_of(res[:, n]), tiles_of(res[:, n])))
                        nc.vector.tensor_tensor(res[:, n], res[:, n], x1[:, n], ALU.add).then_inc(res_ready, 1)


def kernel(**inputs):
    import numpy as np
    import concourse.bacc as bacc
    from concourse.bass_utils import run_bass_kernel_spmd

    a = {k: np.asarray(v) for k, v in inputs.items()}
    arrays = {
        "x": a["L0_attn_x"],
        "wq_lat": a["L0_attn_wq_lat"], "wk_lat": a["L0_attn_wk_lat"], "wv_lat": a["L0_attn_wv_lat"],
        "wq_heads": a["L0_attn_wq_heads"], "wk_heads": a["L0_attn_wk_heads"], "wv_heads": a["L0_attn_wv_heads"],
        "w_proj": a["L0_attn_w_proj"], "b_proj": a["L0_attn_b_proj"],
        "w_fc_t": a["L0_ffn_W_fc"].T,
        "ln_w": a["L0_ffn_ln_w"].reshape(HID // P, P).T, "ln_b": a["L0_ffn_ln_b"].reshape(HID // P, P).T,
        "w_out_t": a["L0_ffn_W_proj"].T,
    }
    arrays = {k: np.ascontiguousarray(v) for k, v in arrays.items()}
    nc = bacc.Bacc("TRN2", target_bir_lowering=False, num_devices=1)
    ap = {k: nc.dram_tensor(f"in_{k}", v.shape, mybir.dt.from_np(v.dtype), kind="ExternalInput").ap()
          for k, v in arrays.items()}
    out = nc.dram_tensor("out", (B, T, C), F32, kind="ExternalOutput").ap()
    block_kernel(nc, ap["x"], (ap["wq_lat"], ap["wk_lat"], ap["wv_lat"]),
                 (ap["wq_heads"], ap["wk_heads"], ap["wv_heads"]), ap["w_proj"], ap["b_proj"],
                 ap["w_fc_t"], ap["ln_w"], ap["ln_b"], ap["w_out_t"], out)
    r = run_bass_kernel_spmd(nc, [{f"in_{k}": v for k, v in arrays.items()}], core_ids=[0])
    return r.results[0]["out"]
```

```python
from contextlib import ExitStack

import concourse.bass as bass
from concourse import mybir

ALU = mybir.AluOpType
ACT = mybir.ActivationFunctionType
AX = mybir.AxisListType
F32 = mybir.dt.float32
BF16 = mybir.dt.bfloat16
U32 = mybir.dt.uint32

P = 128
B, T, C = 2, 1024, 128
LAT = 32
NH, HD = 16, 8
HID = 512
NT = T // P
QUAD = 4
NQ = NH // QUAD
HALF = T // 2
HT = HALF // P
SCALE = HD ** -0.5
LN_EPS = 1e-5
GAMMA_EPS = 1e-6
MASKED = -3.0e38
ONES16 = 0x3F803F80
ROWS = 96
SHIFT_ROW = 64
STACKS = 3
PGROUPS = 4

Q_PARTS = (0, 0, 0, 1, 1, 2)
K_PARTS = (0, 1, 2, 0, 1, 0)
TERMS = len(Q_PARTS)
PART_ROWS = HD * TERMS
STACK_DMAS = 2 * TERMS + 1

def score_groups():
    nb = HALF // P
    groups = []
    for c in range(2):
        for kb in range(nb * c):
            groups.append((c, [(kb, HALF * c, HALF, 0)], 1))
        d, e = nb * c, HALF * (c + 1)
        groups.append((c, [(d, P * d, HALF, 0)], 1))
        groups.append((c, [(d + 1, P * (d + 1), 3 * P, P), (d + 3, P * (d + 3), P, 0)], 1))
        groups.append((c, [(d + 2, P * (d + 2), 2 * P, 0)], 2))
    return groups


GROUPS = score_groups()
UNITS = [(g, tuple(range(i, i + GROUPS[g][2]))) for g in range(len(GROUPS)) for i in range(0, QUAD, GROUPS[g][2])]
NU = len(UNITS)
GROUP_END = [max(u for u, (g, _) in enumerate(UNITS) if g == j) for j in range(len(GROUPS))]
HALF_END = [max(j for j, x in enumerate(GROUPS) if x[0] == c) for c in range(2)]

MAX_TILES = [(0, (0, 1, 2, 3)), (1, (0, 1, 2, 3)), (2, (0, 1)), (2, (2, 3)), (3, (0, 1)), (3, (2, 3))]
MAX_TILES += [(i, (h,)) for i in range(4, NT) for h in range(QUAD)]

WARM_UP = 60
PV_LAG = 5
QUADS = B * NQ

LAST_PAIR = (QUADS - 2, QUADS - 1)
HALVES = [(n, c) for n in range(QUADS - 2) for c in range(2)] + [(n, c) for c in range(2) for n in LAST_PAIR]
SEQUENCE = [(n, u) for n, c in HALVES for u in range(NU) if GROUPS[UNITS[u][0]][0] == c]
STEPS = len(SEQUENCE)
STEP_OF = {x: i for i, x in enumerate(SEQUENCE)}
HALF_NO = {x: i for i, x in enumerate(HALVES)}
GROUP_NO = {x: i for i, x in enumerate((n, g) for n, u in SEQUENCE for g in (UNITS[u][0],) if u == GROUP_END[g])}


def last_step(n, g):
    return STEP_OF[n, GROUP_END[g]]


MAX_SPAN = 33
EARLY_SPAN, LATE_SPAN = 12, 28
LEAD = 10
NORM_SLOTS = 8

BLOCKS = ((0, 0, 4, 0, 1.3), (0, 4, 4, 35, 1.3), (1, 0, 4, 0, 0.7), (1, 4, 2, 0, 0.4), (1, 6, 1, 2, 0.4),
          (1, 7, 1, 4, 0.4))
AFTER = ("yT", "proj", "attn_norm", "x1", "x1_norm", "x1T", "ffn1", "g_stats", "g_norm", "hT", "ffn2", "out_norm",
         "out")
STAGE_STEPS = (0, 4, 10, 13, 19, 22, 26, 31, 36, 41, 47, 53, 56)
STATISTICS = {"ln1_stats": "ln1", "proj": "attn", "x1": "x1", "g_stats": "g", "ffn2": "out"}
BY_TWO_TILES = ("ffn1", "hT")
SCALAR_BLOCKS = (0, 1)


def handovers(n):
    return 2 if n in (0, LAST_PAIR[1]) else 1


def max_steps(n):
    m, early = len(MAX_TILES), len([t for t in MAX_TILES if t[0] < HT])
    if n == 0:
        return [-1] * early + [(k - early) // 2 for k in range(early, m)]
    if n == 1:
        return [8 + k // 3 for k in range(6)] + [10 + k * 21 // (m - 6) for k in range(m - 6)]
    if n == LAST_PAIR[1]:
        first = split_steps(n - 1)[-1] + 1
        return [first + k * EARLY_SPAN // early for k in range(early)] + [
            first + EARLY_SPAN + 7 + k * LATE_SPAN // (m - early) for k in range(m - early)]
    start, end = max((n - 1) * NU - LEAD, split_steps(n - 1)[-1] + 1), (n - 1) * NU - LEAD + MAX_SPAN
    return [start + k * (end - start) // m for k in range(m)]


def split_steps(n):
    if n == 0:
        return (-1, 8)
    early = len([t for t in MAX_TILES if t[0] < HT])
    return tuple(max_steps(n)[k] + 1 for k in ([early - 1] if handovers(n) == 2 else []) + [-1])


def schedule():
    at = {}

    def put(step, *event):
        at.setdefault(max(step, -1), []).append(event)

    def put_input(b, steps):
        for s, kind in zip(steps, ("ln1_stats", "ln1_norm", "xT", "q", "k", "q_part1", "k_part1", "v")):
            put(s, kind, b, 0, 0)

    for kind in ("w_turn", "w_chain", "ln1_stats", "ln1_norm", "xT", "w_abs", "w_sum", "w_ternary", "q", "k", "q_part1",
                 "k_part1", "v", "c2"):
        put(-1, kind, 0, 0, 0)
    for n in range(QUADS):
        for k, step in enumerate(max_steps(n)):
            put(step, "max", 0, n, k)
        for j, step in enumerate(split_steps(n)):
            put(step, "split", 0, n, j)
            put(step + 3 if n else step + j, "ms", 0, n, j)
        for g in range(len(GROUPS)):
            end = last_step(n, g)
            if is_diagonal(g):
                put(end, "mask", 0, n, g)
            put(end + PV_LAG, "values", 0, n, g)
        for c in range(2):
            done = last_step(n, HALF_END[c]) + PV_LAG
            put(done + 1, "take_o", 0, n, c)
            put(done + 4, "o", 0, n, c)
    put_input(1, (38, 42, 46, 54, 58, 60, 62, 66))
    for n, (b, t0, tiles, delay, pace) in enumerate(BLOCKS):
        start = last_step((b + 1) * NQ - 1, HALF_END[t0 // HT]) + PV_LAG + 5 + delay
        for s, kind in zip(STAGE_STEPS, AFTER):
            for k in range((tiles + 1) // 2 if kind in BY_TWO_TILES else 1):
                put(start + int(pace * s), kind, b, n, k)
    return at


def is_diagonal(g):
    return any(P * kb == q0 for kb, q0, _, _ in GROUPS[g][1])


AT = schedule()
LAST = max(AT)

TILE_KINDS = ("w_turn", "w_chain", "xT", "q", "k", "v", "max", "ms", "o", "w_sum", "c2", "yT", "proj", "x1T", "ffn1",
              "hT", "ffn2")
TILE_NO = {e: i for i, e in enumerate(e for s in range(-1, LAST + 1) for e in AT.get(s, ()) if e[0] in TILE_KINDS)}
NORM_NO = {e: i for i, e in enumerate((STATISTICS[e[0]],) + e[1:3] for s in range(-1, LAST + 1)
                                      for e in AT.get(s, ()) if e[0] in STATISTICS)}


def max_place(i, j):
    return (P * (i + 1) if i < 2 else HALF) * j


def block_kernel(nc, x, w_lat, w_heads, w_proj, b_proj, w_fc_t, ln_w, ln_b, w_out_t, out):
    with ExitStack() as ctx:
        def sb(name, shape, dt=F32):
            return ctx.enter_context(nc.sbuf_tensor(name, shape, dt))

        def sem(name):
            return ctx.enter_context(nc.semaphore(name))

        ident = sb("ident", [P, P])
        ident16 = sb("ident16", [P, P], BF16)
        future = sb("future", [P, P], BF16)
        ones = sb("ones", [P, P])
        minus_half = sb("minus_half", [P, NT])
        wlat = sb("wlat", [P, 3 * LAT])
        wheads = sb("wheads", [3 * LAT, 3, C])
        wlatT = sb("wlatT", [3 * LAT, C])
        wqkv = sb("wqkv", [C, 3, C])
        wproj = sb("wproj", [C, C])
        bproj = sb("bproj", [P, C])
        wfc = sb("wfc", [P, HID])
        wfcq = sb("wfcq", [P, HID])
        wout = sb("wout", [P, HID // P, C])
        woutq = sb("woutq", [P, HID // P, C])
        woutl = sb("woutl", [P, HID // P, C])
        lnw = sb("lnw", [P, HID // P])
        lnb = sb("lnb", [P, HID // P])
        lnb_wide = sb("lnb_wide", [P, HID // P, P])
        c2 = sb("c2", [P, C])
        wstat = sb("wstat", [P, 8])

        x_in = sb("x_in", [P, B, NT, C])
        xn = sb("xn", [P, NT, C])
        xnT = sb("xnT", [C, T])
        parts = sb("parts", [P, 2, 3, T], BF16)
        rest = sb("rest", [P, 2, T])
        v_aug = sb("v_aug", [P, B, NT, NH, HD + 1])
        q_stack = sb("q_stack", [ROWS, STACKS, QUAD, T], BF16)
        k_stack = sb("k_stack", [ROWS, STACKS, QUAD, T], BF16)
        neg_max = sb("neg_max", [P, QUAD, NT])
        max_rest = sb("max_rest", [P, QUAD * NT])
        max_parts = sb("max_parts", [P, 3, QUAD * NT], BF16)
        max_rows = sb("max_rows", [3 * QUAD * NT, P], BF16)
        probs = sb("probs", [P, PGROUPS, QUAD * HALF])
        o_cols = sb("o_cols", [P, 2, HALF])
        o_recip = sb("o_recip", [P, 4, QUAD])
        y = sb("y", [P, B, NT, C])
        yT = sb("yT", [C, T])
        x1 = sb("x1", [P, NT, C])
        x1n, x1T = xn, xnT
        gelu = sb("gelu", [P, NT, HID])
        gT = sb("gT", [P, NT, HID // P, P])
        res = sb("res", [P, NT, C])
        stats = sb("stats", [P, NORM_SLOTS, NT, 6])
        mv = sb("mv", [P, NORM_SLOTS, NT, 2])
        veps = sb("veps", [P, NORM_SLOTS, NT])
        negmean = sb("negmean", [P, NORM_SLOTS, NT])
        rstd = sb("rstd", [P, NORM_SLOTS, NT])
        shift = sb("shift", [P, NORM_SLOTS, NT])

        ps = ctx.enter_context(nc.psum_tensor("ps", [P, 8, 512], F32))
        pv = ps[:, 7]

        def work(name):
            return ps[:, 2 * (TILE_NO[name] % 2):2 * (TILE_NO[name] % 2) + 2, :]

        def work_flat(name):
            return work(name).rearrange("p a n -> p (a n)")

        def scores_bank(u):
            return ps[:, 4 + u % 3]

        weights_in = sem("weights_in")
        ternary_in = sem("ternary_in")
        x_in0, x_in1 = sem("x_in0"), sem("x_in1")
        pads_zeroed = sem("pads_zeroed")
        stacks_set = sem("stacks_set")
        ident_ready = sem("ident_ready")
        v_ones = sem("v_ones")
        bank_zeroed = sem("bank_zeroed")
        vec_done = sem("vec_done")
        pool_done = sem("pool_done")
        tile_ready = [sem("tile_ready0"), sem("tile_ready1")]
        tile_free = [sem("tile_free0"), sem("tile_free1")]
        w_abs_ready = sem("w_abs_ready")
        ternary_ready = sem("ternary_ready")
        var_ready = sem("var_ready")
        rstd_ready = sem("rstd_ready")
        attn_centred = sem("attn_centred")
        out_centred = sem("out_centred")
        xn_ready = sem("xn_ready")
        part0_ready = sem("part0_ready")
        part1_ready = sem("part1_ready")
        part2_ready = sem("part2_ready")
        stack_in = [sem(f"stack_in{i}") for i in range(STACKS)]
        max_split = sem("max_split")
        shift_in = sem("shift_in")
        scores_ready = sem("scores_ready")
        exp_done = sem("exp_done")
        masked = sem("masked")
        pv_done = sem("pv_done")
        o_ready = sem("o_ready")
        x1n_ready = [sem(f"x1n_ready{n}") for n in range(len(BLOCKS))]
        gn_ready = [sem(f"gn_ready{n}") for n in range(len(BLOCKS))]
        res_ready = sem("res_ready")
        stored = [sem("stored0"), sem("stored1")]
        block_tiles = [range(t0, t0 + tiles) for _, t0, tiles, _, _ in BLOCKS]

        mask_no = {x: i for i, x in enumerate(x for x in GROUP_NO if is_diagonal(x[1]))}

        def filled(eng, name):
            i = TILE_NO[name]
            eng.wait_ge(tile_ready[i % 2], i // 2 + 1)

        def emptied(eng, name):
            i = TILE_NO[name]
            eng.wait_ge(tile_free[i % 2], i // 2 + 1)

        def release(ins, name):
            ins.then_inc(tile_free[TILE_NO[name] % 2], 1)

        def handed_over(n, j):
            return sum(handovers(i) for i in range(n)) + j + 1

        def half_name(k):
            return ("o", 0) + HALVES[k]

        def on_scalar(kind, b, n):
            return b == 1 if kind == "ln1" else n in SCALAR_BLOCKS

        block = ctx.enter_context(nc.Block())

        @block.sync
        def _(sp):
            for b, arrived in enumerate((x_in0, x_in1)):
                sp.dma_start(x_in[:, b], x[b].rearrange("(t p) c -> p t c", p=P)).then_inc(arrived, 16)
            for i in range(3):
                sp.dma_start(wlat[:, LAT * i:LAT * (i + 1)], w_lat[i]).then_inc(weights_in, 16)
            sp.wait_ge(pads_zeroed, 1)
            for i in range(3):
                sp.dma_start(wheads[LAT * i:LAT * (i + 1), i, :], w_heads[i]).then_inc(weights_in, 16)
            sp.dma_start(wfc[:, :], w_fc_t).then_inc(ternary_in, 16)
            sp.dma_start(wout[:, :, :], w_out_t.rearrange("(c p) d -> p c d", p=P)).then_inc(ternary_in, 16)
            sp.dma_start(lnw[:, :], ln_w).then_inc(ternary_in, 16)
            sp.dma_start(lnb[:, :], ln_b).then_inc(ternary_in, 16)
            sp.dma_start(wproj[:, :], w_proj).then_inc(ternary_in, 16)
            sp.dma_start(bproj[:, :], b_proj.rearrange("(a c) -> a c", a=1).to_broadcast([P, C])
                         ).then_inc(ternary_in, 16)

            def load_stacks(n):
                s, b = n % STACKS, n // NQ
                if n >= STACKS:
                    sp.wait_ge(scores_ready, max(STEP_OF[n - STACKS, u] for u in range(NU)) + 1)
                sp.wait_ge(stacks_set, min(n + 1, STACKS))
                sp.dma_start(q_stack[SHIFT_ROW:SHIFT_ROW + 3, s], k_stack[PART_ROWS:PART_ROWS + 3, s]
                             ).then_inc(stack_in[s], 16)
                channels = slice(QUAD * HD * (n % NQ), QUAD * HD * (n % NQ + 1))
                for r, ready in enumerate((part0_ready, part1_ready, part2_ready)):
                    for a, (stack, term_parts) in enumerate(((q_stack, Q_PARTS), (k_stack, K_PARTS))):
                        sp.wait_ge(ready, 2 * b + a + 1)
                        for i in [i for i in range(TERMS) if term_parts[i] == r]:
                            sp.dma_start(stack[HD * i:HD * (i + 1), s], parts[channels, a, r, :]
                                         ).then_inc(stack_in[s], 16)

            def store_shift(n, j):
                emptied(sp, ("ms", 0, n, j))
                sp.dma_start(q_stack[SHIFT_ROW:SHIFT_ROW + 3, n % STACKS].rearrange("a h (i q) -> a (h i) q", q=P),
                             max_rows[:, :]).then_inc(shift_in, 16)

            load_stacks(0)
            load_stacks(1)
            for s in range(-1, LAST + 1):
                for kind, b, n, k in AT.get(s, ()):
                    if kind == "ms":
                        store_shift(n, k)
                        if k + 1 == handovers(n) and n + 2 < QUADS:
                            load_stacks(n + 2)
                    elif kind == "out":
                        t0, t1 = block_tiles[n][0], block_tiles[n][-1] + 1
                        sp.wait_ge(res_ready, n + 1)
                        sp.dma_start(out[b].rearrange("(t p) c -> p t c", p=P)[:, t0:t1], res[:, t0:t1]
                                     ).then_inc(stored[t0 // HT], 16)
            for h, half in enumerate(stored):
                sp.wait_ge(half, 16 * len([1 for block in BLOCKS if block[1] // HT == h]))

        @block.gpsimd
        def _(pool):
            steps_done = [0]

            def then_wait(ins):
                steps_done[0] += 1
                ins.then_inc(pool_done, 1)
                pool.wait_ge(pool_done, steps_done[0])

            nc.gpsimd.memset(wheads[:, :, :], 0.0).then_inc(pads_zeroed, 1)
            nc.gpsimd.memset(minus_half[:, :], -0.5)
            nc.gpsimd.memset(ident[:, :], 0.0)
            nc.gpsimd.memset(ident16[:, :], 0.0)
            then_wait(nc.gpsimd.memset(future[:, :], 0.0))
            for t in (ident, ident16):
                nc.gpsimd.affine_select(out=t[:, :], in_=t[:, :], compare_op=ALU.not_equal, fill=1.0, base=0,
                                        pattern=[[-1, P]], channel_multiplier=1).then_inc(ident_ready, 1)
            nc.gpsimd.affine_select(out=future[:, :], in_=future[:, :], compare_op=ALU.is_ge, fill=MASKED, base=0,
                                    pattern=[[-1, P]], channel_multiplier=1).then_inc(ident_ready, 1)

            def inverse_std(which):
                k, m = NORM_NO[which], NT if which[0] == "ln1" else len(block_tiles[which[2]])
                slot = k % NORM_SLOTS
                pool.wait_ge(var_ready, k + 1)
                ins = nc.gpsimd.tensor_tensor(rstd[:, slot, 0:m], veps[:, slot, 0:m], minus_half[:, 0:m], ALU.pow)
                if on_scalar(*which):
                    then_wait(ins)
                    ins = nc.gpsimd.tensor_tensor(shift[:, slot, 0:m], negmean[:, slot, 0:m], rstd[:, slot, 0:m],
                                                  ALU.mult)
                ins.then_inc(rstd_ready, 1)

            def last_part(b, a):
                pool.wait_ge(part1_ready, 2 * b + a + 1)
                nc.gpsimd.tensor_tensor(parts[:, a, 2, :], rest[:, a, :], parts[:, a, 1, :],
                                        ALU.subtract).then_inc(part2_ready, 1)

            def mask(n, g):
                _, pieces, per = GROUPS[g]
                pool.wait_ge(exp_done, last_step(n, g) + 1)
                buf = probs[:, GROUP_NO[n, g] % PGROUPS, :]
                share = HALF // per
                v = buf[:, 0:QUAD * share].rearrange("p (h q) -> p h q", h=QUAD)[:, :, 0:len(pieces) * P]
                nc.gpsimd.affine_select(out=v, in_=v, compare_op=ALU.is_ge, fill=0.0, base=0,
                                        pattern=[[0, QUAD], [0, len(pieces)], [1, P]][:: 1 if len(pieces) > 1 else 2],
                                        channel_multiplier=-1).then_inc(masked, 1)

            for s in range(-1, LAST + 1):
                for kind, b, n, k in AT.get(s, ()):
                    if kind in STATISTICS:
                        inverse_std((STATISTICS[kind], b, n))
                        if s < 0:
                            for i in range(STACKS):
                                q_words, k_words = (t[:, i].rearrange("r h t -> r (h t)").bitcast(U32)
                                                    for t in (q_stack, k_stack))
                                nc.gpsimd.memset(q_words, 0)
                                then_wait(nc.gpsimd.memset(k_words, 0))
                                nc.gpsimd.memset(k_words[SHIFT_ROW:SHIFT_ROW + 3], ONES16).then_inc(stacks_set, 1)
                                pool.wait_ge(stacks_set, i + 1)
                    elif kind in ("q_part1", "k_part1") and b:
                        last_part(b, "qk".index(kind[0]))
                    elif kind == "mask":
                        mask(n, k)

        @block.tensor
        def _(pe):
            def claim(name):
                i = TILE_NO[name]
                if i >= 2:
                    pe.wait_ge(tile_free[i % 2], i // 2)
                return work_flat(name)

            def fill_done(ins, name):
                ins.then_inc(tile_ready[TILE_NO[name] % 2], 1)

            def turn_tiles(name, tiles):
                w = claim(name)
                for t, src in enumerate(tiles):
                    mm = pe.transpose(w[:, P * t:P * (t + 1)], src, ident[:, :])
                fill_done(mm, name)

            def project(name, lhs, rhs):
                w = claim(name)
                for c in range(2):
                    mm = pe.matmul(w[0:lhs.free_size(), HALF * c:HALF * (c + 1)], lhs, rhs[:, HALF * c:HALF * (c + 1)],
                                   start=True, stop=True)
                fill_done(mm, name)

            def by_token(name, lhsT, rhs, tiles):
                w = claim(name)
                m = rhs.shape[1]
                for i, t in enumerate(tiles):
                    mm = pe.matmul(w[:, m * i:m * (i + 1)], lhsT[:, P * t:P * (t + 1)], rhs, start=True, stop=True)
                fill_done(mm, name)

            def max_tile(n, k):
                name = ("max", 0, n, k)
                i, heads = MAX_TILES[k]
                s = n % STACKS
                if handovers(n) == 2 and i == HT and heads[0] == 0:
                    pe.wait_ge(shift_in, 16 * handed_over(n, 0))
                if k == 0:
                    pe.wait_ge(stack_in[s], 16 * STACK_DMAS * (n // STACKS + 1))
                w = claim(name)
                width = P * (i + 1)
                for j, h in enumerate(heads):
                    at = max_place(i, j)
                    lhs = q_stack[:, s, h, P * i:P * (i + 1)]
                    for k0 in range(0, width, 512):
                        kw = min(512, width - k0)
                        mm = pe.matmul(w[:, at + k0:at + k0 + kw], lhs, k_stack[:, s, h, k0:k0 + kw],
                                       start=True, stop=k0 + kw != width)
                    mm = pe.matmul(w[:, at + width - P:at + width], ident16[:, :], future[:, :],
                                   start=False, stop=True)
                fill_done(mm, name)

            def max_turn(n, j):
                name = ("ms", 0, n, j)
                pe.wait_ge(max_split, handed_over(n, j))
                w = claim(name)
                mm = pe.transpose(w.bitcast(BF16)[0:3 * QUAD * NT, 0:P],
                                  max_parts[:, :, :].rearrange("p a n -> p (a n)"), ident16[:, :])
                fill_done(mm, name)

            def scores_unit(n, u):
                g, heads = UNITS[u]
                cnt = STEP_OF[n, u]
                if u == 0:
                    pe.wait_ge(shift_in, 16 * handed_over(n, 0))
                elif handovers(n) == 2 and g > HALF_END[0]:
                    pe.wait_ge(shift_in, 16 * handed_over(n, 1))
                if cnt >= 3:
                    pe.wait_ge(exp_done, cnt - 2)
                bank = scores_bank(cnt)
                s = n % STACKS
                for j, h in enumerate(heads):
                    for kb, q0, w, at in GROUPS[g][1]:
                        at += j * (HALF // len(heads))
                        mm = pe.matmul(bank[:, at:at + w], k_stack[:, s, h, P * kb:P * (kb + 1)],
                                       q_stack[:, s, h, q0:q0 + w], start=True, stop=True)
                mm.then_inc(scores_ready, 1)

            def values(n, g):
                c, pieces, per = GROUPS[g]
                pe.wait_ge(exp_done, last_step(n, g) + 1)
                if (n, g) in mask_no:
                    pe.wait_ge(masked, mask_no[n, g] + 1)
                if n % NQ == 0 and g == 0:
                    emptied(pe, ("v", n // NQ, 0, 0))
                first, last = pieces[0][0] == 0, g == HALF_END[c]
                if first and HALF_NO[n, c]:
                    pe.wait_ge(o_ready, HALF_NO[n, c])
                buf = probs[:, GROUP_NO[n, g] % PGROUPS, :]
                for kb, q0, w, at in pieces:
                    for h in range(QUAD):
                        a = h * (HALF // per) + at
                        mm = pe.matmul(pv[32 * h:32 * h + HD + 1, q0 - HALF * c:q0 - HALF * c + w],
                                       v_aug[:, n // NQ, kb, QUAD * (n % NQ) + h, :], buf[:, a:a + w],
                                       start=first, stop=last)
                mm.then_inc(pv_done, 1)

            def turn_o(n, c):
                k = HALF_NO[n, c]
                pe.wait_ge(o_ready, k + 1)
                turn_tiles(("o", 0, n, c), [o_cols[:, k % 2, P * t:P * (t + 1)] for t in range(HT)])

            pe.wait_ge(ident_ready, 3)
            for _ in range(WARM_UP):
                pe.transpose(scores_bank(0).bitcast(BF16)[:, 0:P], ident16[:, :], ident16[:, :])
            pe.wait_ge(bank_zeroed, 1)
            pe.wait_ge(v_ones, 1)
            for s in range(-1, LAST + 1):
                if 0 <= s < STEPS:
                    scores_unit(*SEQUENCE[s])
                for kind, b, n, k in AT.get(s, ()):
                    name = (kind, b, n, k)
                    if kind == "max":
                        max_tile(n, k)
                    elif kind == "ms":
                        max_turn(n, k)
                    elif kind == "values":
                        values(n, k)
                    elif kind == "o":
                        turn_o(n, k)
                    elif kind == "xT":
                        pe.wait_ge(xn_ready, b + 1)
                        turn_tiles(name, [xn[:, t, :] for t in range(NT)])
                    elif kind == "w_turn":
                        pe.wait_ge(weights_in, 96)
                        w = claim(name)
                        fill_done(pe.transpose(w[0:3 * LAT, 0:C], wlat[:, :], ident[:, :]), name)
                    elif kind == "w_chain":
                        emptied(pe, ("w_turn", 0, 0, 0))
                        w = claim(name)
                        for i in range(3):
                            mm = pe.matmul(w[:, C * i:C * (i + 1)], wlatT[:, :], wheads[:, i, :], start=True,
                                           stop=True)
                        fill_done(mm, name)
                    elif kind in ("q", "k"):
                        emptied(pe, ("w_chain", 0, 0, 0))
                        emptied(pe, ("xT", b, 0, 0))
                        project(name, wqkv[:, "qk".index(kind), :], xnT)
                    elif kind == "v":
                        by_token(name, xnT, wqkv[:, 2, :], range(NT))
                    elif kind == "w_sum":
                        pe.wait_ge(w_abs_ready, 1)
                        w = claim(name)
                        fill_done(pe.matmul(w[:, 0:2], ones[:, :], wstat[:, 0:2], start=True, stop=True), name)
                    elif kind == "c2":
                        pe.wait_ge(ternary_ready, 1)
                        w = claim(name)
                        for c in range(HID // P):
                            mm = pe.matmul(w[:, 0:C], lnb_wide[:, c, :], woutq[:, c, :], start=c == 0,
                                           stop=c == HID // P - 1)
                        fill_done(mm, name)
                    elif kind == "yT":
                        emptied(pe, ("o", 0, NQ * (b + 1) - 1, block_tiles[n][0] // HT))
                        turn_tiles(name, [y[:, b, t, :] for t in block_tiles[n]])
                    elif kind == "proj":
                        emptied(pe, ("yT", b, n, 0))
                        by_token(name, yT, wproj[:, :], block_tiles[n])
                    elif kind == "x1T":
                        pe.wait_ge(x1n_ready[n], 1)
                        turn_tiles(name, [x1n[:, t, :] for t in block_tiles[n]])
                    elif kind == "ffn1":
                        emptied(pe, ("x1T", b, n, 0))
                        by_token(name, x1T, wfcq[:, :], block_tiles[n][2 * k:2 * k + 2])
                    elif kind == "hT":
                        pe.wait_ge(gn_ready[n], min(2 * k + 2, len(block_tiles[n])))
                        turn_tiles(name, [gelu[:, t, P * j:P * (j + 1)] for t in block_tiles[n][2 * k:2 * k + 2]
                                          for j in range(HID // P)])
                    elif kind == "ffn2":
                        w = claim(name)
                        for i, t in enumerate(block_tiles[n]):
                            if i % 2 == 0:
                                emptied(pe, ("hT", b, n, i // 2))
                            for c in range(HID // P):
                                mm = pe.matmul(w[:, P * i:P * (i + 1)], gT[:, t, c, :], woutl[:, c, :],
                                               start=c == 0, stop=c == HID // P - 1)
                        fill_done(mm, name)

        @block.scalar
        def _(act):
            def exponentials(n, u):
                g, _ = UNITS[u]
                cnt, group = STEP_OF[n, u], GROUP_NO[n, g]
                act.wait_ge(scores_ready, cnt + 1)
                if group >= PGROUPS:
                    act.wait_ge(pv_done, group - PGROUPS + 1)
                at = (u - (GROUP_END[g - 1] + 1 if g else 0)) * HALF
                nc.scalar.activation(probs[:, group % PGROUPS, at:at + HALF], scores_bank(cnt), ACT.Exp,
                                     scale=SCALE).then_inc(exp_done, 1)

            def take_o(n, c):
                k = HALF_NO[n, c]
                act.wait_ge(pv_done, GROUP_NO[n, HALF_END[c]] + 1)
                if k >= 2:
                    filled(act, half_name(k - 2))
                nc.scalar.copy(o_cols[:, k % 2, :], pv).then_inc(o_ready, 1)

            def copy_tile(dst, name, rows=P):
                filled(act, name)
                src = work_flat(name)[0:rows, 0:dst.free_size()]
                release(nc.scalar.copy(dst, src), name)

            def normalise(which, dst, src):
                act.wait_ge(rstd_ready, NORM_NO[which] + 1)
                slot = NORM_NO[which] % NORM_SLOTS
                return [nc.scalar.activation(dst[t], src[t], ACT.Identity, bias=shift[:, slot, t:t + 1],
                                             scale=rstd[:, slot, t:t + 1]) for t in range(len(src))]

            def each(buffer, n):
                return [buffer[:, t, :] for t in block_tiles[n]]

            for s in range(-1, LAST + 1):
                if 0 <= s < STEPS:
                    exponentials(*SEQUENCE[s])
                for kind, b, n, k in AT.get(s, ()):
                    name = (kind, b, n, k)
                    tiles = block_tiles[n] if kind in AFTER else ()
                    if kind == "take_o":
                        take_o(n, k)
                    elif kind == "xT":
                        copy_tile(xnT[:, :], name)
                    elif kind == "w_turn":
                        copy_tile(wlatT[:, :], name, 3 * LAT)
                    elif kind == "w_chain":
                        filled(act, name)
                        w = work_flat(name)[:, 0:3 * C].rearrange("c (i q h d) -> c i q h d", i=3, q=NQ, h=QUAD)
                        for i in range(2):
                            nc.scalar.copy(wqkv[:, i, :].rearrange("c (q d h) -> c q h d", q=NQ, h=QUAD), w[:, i])
                        release(nc.scalar.copy(wqkv[:, 2, :], work_flat(name)[:, 2 * C:3 * C]), name)
                    elif kind in ("q", "k"):
                        if b and kind == "q":
                            act.wait_ge(stack_in[(NQ - 1) % STACKS], 16 * STACK_DMAS * ((NQ - 1) // STACKS + 1))
                        filled(act, name)
                        nc.scalar.copy(parts[:, "qk".index(kind), 0, :], work_flat(name)).then_inc(part0_ready, 1)
                    elif kind in ("q_part1", "k_part1"):
                        a = "qk".index(kind[0])
                        emptied(act, (kind[0], b, 0, 0))
                        nc.scalar.copy(parts[:, a, 1, :], rest[:, a, :]).then_inc(part1_ready, 1)
                    elif kind == "v":
                        filled(act, name)
                        release(nc.scalar.copy(v_aug[:, b, :, :, 0:HD],
                                               work_flat(name).rearrange("p (t h d) -> p t h d", t=NT, h=NH)), name)
                    elif kind == "ln1_norm" and on_scalar("ln1", b, n):
                        normalise(("ln1", b, 0), [xn[:, t, :] for t in range(NT)],
                                  [x_in[:, b, t, :] for t in range(NT)])[-1].then_inc(xn_ready, 1)
                    elif kind.endswith("_norm") and kind != "ln1_norm" and on_scalar(kind[:-5], b, n):
                        if kind == "x1_norm":
                            normalise(("x1", b, n), each(x1n, n), each(x1, n))[-1].then_inc(x1n_ready[n], 1)
                        elif kind == "g_norm":
                            for ins in normalise(("g", b, n), each(gelu, n), each(gelu, n)):
                                ins.then_inc(gn_ready[n], 1)
                        else:
                            normalise((kind[:-5], b, n), each(res, n), each(res, n))[-1].then_inc(
                                attn_centred if kind == "attn_norm" else out_centred, 1)
                    elif kind == "yT":
                        copy_tile(yT[:, P * tiles[0]:P * (tiles[-1] + 1)], name)
                    elif kind == "x1T":
                        copy_tile(x1T[:, P * tiles[0]:P * (tiles[-1] + 1)], name)
                    elif kind == "ffn1":
                        filled(act, name)
                        pair = tiles[2 * k:2 * k + 2]
                        release(nc.scalar.activation(gelu[:, pair[0]:pair[-1] + 1, :], work(name)[:, 0:len(pair), :],
                                                      ACT.Gelu), name)
                    elif kind == "hT":
                        pair = tiles[2 * k:2 * k + 2]
                        copy_tile(gT[:, pair[0]:pair[-1] + 1].rearrange("p t c q -> p (t c q)"), name)

        @block.vector
        def _(vec):
            steps_done = [0]

            def then_wait(ins):
                steps_done[0] += 1
                ins.then_inc(vec_done, 1)
                vec.wait_ge(vec_done, steps_done[0])

            def statistics(which, tiles):
                k = NORM_NO[which] % NORM_SLOTS
                for t, src in enumerate(tiles):
                    ins = nc.vector.bn_stats(stats[:, k, t, :], src)
                then_wait(ins)
                for t in range(len(tiles)):
                    ins = nc.vector.bn_aggr(mv[:, k, t, :], stats[:, k, t, :])
                then_wait(ins)
                if on_scalar(*which):
                    nc.vector.tensor_scalar(negmean[:, k, 0:len(tiles)], mv[:, k, 0:len(tiles), 0], -1.0, None,
                                            ALU.mult)
                nc.vector.tensor_scalar(veps[:, k, 0:len(tiles)], mv[:, k, 0:len(tiles), 1], LN_EPS, None, ALU.add
                                        ).then_inc(var_ready, 1)

            def normalise(which, dst, src):
                vec.wait_ge(rstd_ready, NORM_NO[which] + 1)
                slot = NORM_NO[which] % NORM_SLOTS
                for t in range(len(src)):
                    ins = nc.vector.tensor_scalar(dst[t], src[t], mv[:, slot, t, 0:1], rstd[:, slot, t:t + 1],
                                                  ALU.subtract, ALU.mult)
                return ins

            def row_maxima(n, k):
                name = ("max", 0, n, k)
                i, heads = MAX_TILES[k]
                width = P * (i + 1)
                if k == 0 and handovers(n) == 2:
                    nc.vector.memset(neg_max[:, :, HT:NT], 0.0)
                filled(vec, name)
                w = work_flat(name)
                if len(heads) == 1:
                    src, dst = w[:, 0:width], neg_max[:, heads[0], i:i + 1]
                else:
                    stride = max_place(i, 1)
                    src = w[:, 0:stride * len(heads)].rearrange("p (h k) -> p h k", k=stride)[:, :, 0:width]
                    dst = neg_max[:, heads[0]:heads[-1] + 1, i]
                release(nc.vector.tensor_reduce(dst, src, AX.X, ALU.max, negate=True), name)

            def split_maxima(n, j):
                blocks = range(HT) if j + 1 < handovers(n) else range(NT)
                names = [("max", 0, n, k) for k, t in enumerate(MAX_TILES) if t[0] in blocks]
                for name in {TILE_NO[name] % 2: name for name in names}.values():
                    emptied(vec, name)
                flat = neg_max[:, :, :].rearrange("p h i -> p (h i)")
                then_wait(nc.vector.tensor_copy(max_parts[:, 0, :], flat))
                then_wait(nc.vector.tensor_tensor(max_rest[:, :], flat, max_parts[:, 0, :], ALU.subtract))
                then_wait(nc.vector.tensor_copy(max_parts[:, 1, :], max_rest[:, :]))
                nc.vector.tensor_tensor(max_parts[:, 2, :], max_rest[:, :], max_parts[:, 1, :],
                                        ALU.subtract).then_inc(max_split, 1)

            def rows_of_maxima(n, j):
                name = ("ms", 0, n, j)
                filled(vec, name)
                if n or j:
                    vec.wait_ge(shift_in, 16 * (handed_over(n, j) - 1))
                release(nc.vector.tensor_copy(max_rows[:, :], work_flat(name).bitcast(BF16)[0:3 * QUAD * NT, 0:P]),
                        name)

            def divide(n, c):
                name = ("o", 0, n, c)
                filled(vec, name)
                w = work_flat(name)[:, 0:HT * P].rearrange("p (t h e) -> p t h e", t=HT, h=QUAD)
                if HALF_NO[n, c]:
                    emptied(vec, half_name(HALF_NO[n, c] - 1))
                then_wait(nc.vector.reciprocal(o_recip[:, :, :], w[:, :, :, HD]))
                m = QUAD * HD
                dst = y[:, n // NQ, HT * c:HT * (c + 1), m * (n % NQ):m * (n % NQ + 1)].rearrange("p t (h d) -> p t h d", d=HD)
                release(nc.vector.tensor_tensor(dst, w[:, :, :, 0:HD],
                                                o_recip[:, :, :].unsqueeze(3).to_broadcast([P, HT, QUAD, HD]),
                                                ALU.mult), name)

            def add_bias(name, dst, bias):
                filled(vec, name)
                m = dst.shape[1]
                release(nc.vector.tensor_tensor(dst, work_flat(name)[:, 0:C * m].rearrange("p (t c) -> p t c", t=m),
                                                bias.unsqueeze(1).to_broadcast([P, m, C]), ALU.add), name)
                emptied(vec, name)

            def each(buffer, n):
                return [buffer[:, t, :] for t in block_tiles[n]]

            wtmp = gelu[:, 0, :]
            wout_flat = wout[:, :, :].rearrange("p c d -> p (c d)")
            woutq_flat = woutq[:, :, :].rearrange("p c d -> p (c d)")

            nc.vector.memset(pv, 0.0).then_inc(bank_zeroed, 1)
            nc.vector.memset(v_aug[:, :, :, :, HD:HD + 1].rearrange("p b t h e -> p (b t h) e"), 1.0
                             ).then_inc(v_ones, 1)
            for s in range(-1, LAST + 1):
                for kind, b, n, k in AT.get(s, ()):
                    name = (kind, b, n, k)
                    if kind in AFTER:
                        own = slice(block_tiles[n][0], block_tiles[n][-1] + 1)
                    if kind == "max":
                        row_maxima(n, k)
                    elif kind == "split":
                        split_maxima(n, k)
                    elif kind == "ms":
                        rows_of_maxima(n, k)
                    elif kind == "o":
                        divide(n, k)
                    elif kind == "ln1_stats":
                        vec.wait_ge(x_in1 if b else x_in0, 16)
                        statistics(("ln1", b, 0), [x_in[:, b, t, :] for t in range(NT)])
                        if b == 0:
                            nc.vector.memset(ones[:, :], 1.0)
                    elif kind.endswith("_norm") and on_scalar(kind[:-5], b, n):
                        pass
                    elif kind == "ln1_norm":
                        normalise(("ln1", b, 0), [xn[:, t, :] for t in range(NT)],
                                  [x_in[:, b, t, :] for t in range(NT)]).then_inc(xn_ready, 1)
                    elif kind in ("q", "k"):
                        a = "qk".index(kind)
                        filled(vec, name)
                        vec.wait_ge(part0_ready, 2 * b + a + 1)
                        release(nc.vector.tensor_tensor(rest[:, a, :], work_flat(name), parts[:, a, 0, :],
                                                        ALU.subtract), name)
                    elif kind in ("q_part1", "k_part1") and b == 0:
                        a = "qk".index(kind[0])
                        vec.wait_ge(part1_ready, a + 1)
                        nc.vector.tensor_tensor(parts[:, a, 2, :], rest[:, a, :], parts[:, a, 1, :],
                                                ALU.subtract).then_inc(part2_ready, 1)
                    elif kind == "w_abs":
                        vec.wait_ge(ternary_in, 96)
                        nc.vector.tensor_reduce(wstat[:, 0:1], wfc[:, :], AX.X, ALU.add, apply_absolute_value=True)
                        nc.vector.tensor_reduce(wstat[:, 1:2], wout_flat, AX.X, ALU.add,
                                                apply_absolute_value=True).then_inc(w_abs_ready, 1)
                    elif kind == "w_sum":
                        filled(vec, name)
                        release(nc.vector.tensor_scalar(wstat[:, 2:4], work_flat(name)[:, 0:2], 1.0 / (HID * C),
                                                        GAMMA_EPS, ALU.mult, ALU.add), name)
                        emptied(vec, name)
                        then_wait(nc.vector.reciprocal(wstat[:, 4:6], wstat[:, 2:4]))
                    elif kind == "w_ternary":
                        for j, (src, dst) in enumerate(((wfc[:, :], wfcq[:, :]), (wout_flat, woutq_flat))):
                            gamma = wstat[:, 4 + j:5 + j]
                            nc.vector.tensor_scalar(dst, src, gamma, 0.5, ALU.mult, ALU.is_gt)
                            then_wait(nc.vector.tensor_scalar(wtmp, src, gamma, -0.5, ALU.mult, ALU.is_lt))
                            then_wait(nc.vector.tensor_tensor(dst, dst, wtmp, ALU.subtract))
                        for c in range(HID // P):
                            nc.vector.tensor_scalar(woutl[:, c, :], woutq[:, c, :], lnw[:, c:c + 1], None, ALU.mult)
                            ins = nc.vector.tensor_scalar(lnb_wide[:, c, :], ones[:, :], lnb[:, c:c + 1], None,
                                                          ALU.mult)
                        ins.then_inc(ternary_ready, 1)
                    elif kind == "c2":
                        filled(vec, name)
                        release(nc.vector.tensor_copy(c2[:, :], work_flat(name)[:, 0:C]), name)
                    elif kind == "proj":
                        if b:
                            vec.wait_ge(stored[block_tiles[n][0] // HT], 16)
                        add_bias(name, res[:, own], bproj[:, :])
                        statistics(("attn", b, n), each(res, n))
                    elif kind in ("attn_norm", "out_norm"):
                        then_wait(normalise((kind[:-5], b, n), each(res, n), each(res, n)))
                    elif kind == "x1":
                        if on_scalar("attn", b, n):
                            vec.wait_ge(attn_centred, SCALAR_BLOCKS.index(n) + 1)
                        then_wait(nc.vector.tensor_tensor(x1[:, own], res[:, own], x_in[:, b, own], ALU.add))
                        statistics(("x1", b, n), each(x1, n))
                    elif kind == "x1_norm":
                        normalise(("x1", b, n), each(x1n, n), each(x1, n)).then_inc(x1n_ready[n], 1)
                    elif kind == "g_stats":
                        for j in range((len(block_tiles[n]) + 1) // 2):
                            emptied(vec, ("ffn1", b, n, j))
                        statistics(("g", b, n), each(gelu, n))
                    elif kind == "g_norm":
                        vec.wait_ge(rstd_ready, NORM_NO["g", b, n] + 1)
                        slot = NORM_NO["g", b, n] % NORM_SLOTS
                        for i, t in enumerate(block_tiles[n]):
                            nc.vector.tensor_scalar(gelu[:, t, :], gelu[:, t, :], mv[:, slot, i, 0:1],
                                                    rstd[:, slot, i:i + 1], ALU.subtract, ALU.mult
                                                    ).then_inc(gn_ready[n], 1)
                    elif kind == "ffn2":
                        add_bias(name, res[:, own], c2[:, :])
                        statistics(("out", b, n), each(res, n))
                    elif kind == "out":
                        if on_scalar("out", b, n):
                            vec.wait_ge(out_centred, SCALAR_BLOCKS.index(n) + 1)
                        nc.vector.tensor_tensor(res[:, own], res[:, own], x1[:, own], ALU.add
                                                ).then_inc(res_ready, 1)


def kernel(**inputs):
    import numpy as np
    import concourse.bacc as bacc
    from concourse.bass_utils import run_bass_kernel_spmd

    a = {k: np.asarray(v) for k, v in inputs.items()}
    arrays = {
        "x": a["L0_attn_x"],
        "wq_lat": a["L0_attn_wq_lat"], "wk_lat": a["L0_attn_wk_lat"], "wv_lat": a["L0_attn_wv_lat"],
        "wq_heads": a["L0_attn_wq_heads"], "wk_heads": a["L0_attn_wk_heads"], "wv_heads": a["L0_attn_wv_heads"],
        "w_proj": a["L0_attn_w_proj"], "b_proj": a["L0_attn_b_proj"],
        "w_fc_t": a["L0_ffn_W_fc"].T,
        "ln_w": a["L0_ffn_ln_w"].reshape(HID // P, P).T, "ln_b": a["L0_ffn_ln_b"].reshape(HID // P, P).T,
        "w_out_t": a["L0_ffn_W_proj"].T,
    }
    arrays = {k: np.ascontiguousarray(v) for k, v in arrays.items()}
    nc = bacc.Bacc("TRN2", target_bir_lowering=False, num_devices=1)
    ap = {k: nc.dram_tensor(f"in_{k}", v.shape, mybir.dt.from_np(v.dtype), kind="ExternalInput").ap()
          for k, v in arrays.items()}
    out = nc.dram_tensor("out", (B, T, C), F32, kind="ExternalOutput").ap()
    block_kernel(nc, ap["x"], (ap["wq_lat"], ap["wk_lat"], ap["wv_lat"]),
                 (ap["wq_heads"], ap["wk_heads"], ap["wv_heads"]), ap["w_proj"], ap["b_proj"],
                 ap["w_fc_t"], ap["ln_w"], ap["ln_b"], ap["w_out_t"], out)
    r = run_bass_kernel_spmd(nc, [{f"in_{k}": v for k, v in arrays.items()}], core_ids=[0])
    return r.results[0]["out"]
```
